# Optimizing a Trainium2 kernel written in Bass

```python
import numpy as np
import jax
import jax.numpy as jnp

def _softmax(x, axis=-1):
    return jax.nn.softmax(x, axis=axis)

def _gelu(x):
    return jax.nn.gelu(x, approximate=True)

def _silu(x):
    return jax.nn.silu(x)

def _sigmoid(x):
    return jax.nn.sigmoid(x)

def _layernorm(x, axis=-1, eps=1e-05):
    m = jnp.mean(x, axis=axis, keepdims=True)
    v = jnp.var(x, axis=axis, keepdims=True)
    return (x - m) / jnp.sqrt(v + eps)

def _scatter_add(tgt, idx, src, axis=0):
    return tgt.at[idx].add(src)

def _segment_sum(src, seg, n):
    return jax.ops.segment_sum(src, seg, n)
kernel_name = 'mk_dlrm_tower_d1_rec_r8_e23449'

def setup_inputs(seed: int=0):
    np.random.seed(seed)
    _w = jnp.asarray

    def _rec_inputs():
        import jax
        import jax.numpy as jnp
        _tk = jax.random.key(seed)
        dense_ctx = jax.random.normal(jax.random.fold_in(_tk, 190), (2048, 16), jnp.float32)
        ids = jnp.stack([jax.random.randint(jax.random.fold_in(_tk, 200 + f), (2048,), 0, v, jnp.int32) for f, v in enumerate([1250, 1250, 125000, 1250, 1000, 1250, 125000, 12500, 125000, 1000, 1250, 125000, 125000, 1000, 1000, 1000, 1000, 125000, 1000, 1250, 1000, 1250, 12500, 1000, 1000, 125000, 12500, 12500, 1250, 125000, 1000, 1250, 1250, 12500, 1000, 1000, 12500, 12500, 12500])], axis=1)
        tbl_0 = 0.05 * jax.random.normal(jax.random.fold_in(_tk, 500 + 0), (1250, 16), jnp.float32)
        tbl_1 = 0.05 * jax.random.normal(jax.random.fold_in(_tk, 500 + 1), (1250, 16), jnp.float32)
        tbl_2 = 0.05 * jax.random.normal(jax.random.fold_in(_tk, 500 + 2), (125000, 16), jnp.float32)
        tbl_3 = 0.05 * jax.random.normal(jax.random.fold_in(_tk, 500 + 3), (1250, 16), jnp.float32)
        tbl_4 = 0.05 * jax.random.normal(jax.random.fold_in(_tk, 500 + 4), (1000, 16), jnp.float32)
        tbl_5 = 0.05 * jax.random.normal(jax.random.fold_in(_tk, 500 + 5), (1250, 16), jnp.float32)
        tbl_6 = 0.05 * jax.random.normal(jax.random.fold_in(_tk, 500 + 6), (125000, 16), jnp.float32)
        tbl_7 = 0.05 * jax.random.normal(jax.random.fold_in(_tk, 500 + 7), (12500, 16), jnp.float32)
        tbl_8 = 0.05 * jax.random.normal(jax.random.fold_in(_tk, 500 + 8), (125000, 16), jnp.float32)
        tbl_9 = 0.05 * jax.random.normal(jax.random.fold_in(_tk, 500 + 9), (1000, 16), jnp.float32)
        tbl_10 = 0.05 * jax.random.normal(jax.random.fold_in(_tk, 500 + 10), (1250, 16), jnp.float32)
        tbl_11 = 0.05 * jax.random.normal(jax.random.fold_in(_tk, 500 + 11), (125000, 16), jnp.float32)
        tbl_12 = 0.05 * jax.random.normal(jax.random.fold_in(_tk, 500 + 12), (125000, 16), jnp.float32)
        tbl_13 = 0.05 * jax.random.normal(jax.random.fold_in(_tk, 500 + 13), (1000, 16), jnp.float32)
        tbl_14 = 0.05 * jax.random.normal(jax.random.fold_in(_tk, 500 + 14), (1000, 16), jnp.float32)
        tbl_15 = 0.05 * jax.random.normal(jax.random.fold_in(_tk, 500 + 15), (1000, 16), jnp.float32)
        tbl_16 = 0.05 * jax.random.normal(jax.random.fold_in(_tk, 500 + 16), (1000, 16), jnp.float32)
        tbl_17 = 0.05 * jax.random.normal(jax.random.fold_in(_tk, 500 + 17), (125000, 16), jnp.float32)
        tbl_18 = 0.05 * jax.random.normal(jax.random.fold_in(_tk, 500 + 18), (1000, 16), jnp.float32)
        tbl_19 = 0.05 * jax.random.normal(jax.random.fold_in(_tk, 500 + 19), (1250, 16), jnp.float32)
        tbl_20 = 0.05 * jax.random.normal(jax.random.fold_in(_tk, 500 + 20), (1000, 16), jnp.float32)
        tbl_21 = 0.05 * jax.random.normal(jax.random.fold_in(_tk, 500 + 21), (1250, 16), jnp.float32)
        tbl_22 = 0.05 * jax.random.normal(jax.random.fold_in(_tk, 500 + 22), (12500, 16), jnp.float32)
        tbl_23 = 0.05 * jax.random.normal(jax.random.fold_in(_tk, 500 + 23), (1000, 16), jnp.float32)
        tbl_24 = 0.05 * jax.random.normal(jax.random.fold_in(_tk, 500 + 24), (1000, 16), jnp.float32)
        tbl_25 = 0.05 * jax.random.normal(jax.random.fold_in(_tk, 500 + 25), (125000, 16), jnp.float32)
        tbl_26 = 0.05 * jax.random.normal(jax.random.fold_in(_tk, 500 + 26), (12500, 16), jnp.float32)
        tbl_27 = 0.05 * jax.random.normal(jax.random.fold_in(_tk, 500 + 27), (12500, 16), jnp.float32)
        tbl_28 = 0.05 * jax.random.normal(jax.random.fold_in(_tk, 500 + 28), (1250, 16), jnp.float32)
        tbl_29 = 0.05 * jax.random.normal(jax.random.fold_in(_tk, 500 + 29), (125000, 16), jnp.float32)
        tbl_30 = 0.05 * jax.random.normal(jax.random.fold_in(_tk, 500 + 30), (1000, 16), jnp.float32)
        tbl_31 = 0.05 * jax.random.normal(jax.random.fold_in(_tk, 500 + 31), (1250, 16), jnp.float32)
        tbl_32 = 0.05 * jax.random.normal(jax.random.fold_in(_tk, 500 + 32), (1250, 16), jnp.float32)
        tbl_33 = 0.05 * jax.random.normal(jax.random.fold_in(_tk, 500 + 33), (12500, 16), jnp.float32)
        tbl_34 = 0.05 * jax.random.normal(jax.random.fold_in(_tk, 500 + 34), (1000, 16), jnp.float32)
        tbl_35 = 0.05 * jax.random.normal(jax.random.fold_in(_tk, 500 + 35), (1000, 16), jnp.float32)
        tbl_36 = 0.05 * jax.random.normal(jax.random.fold_in(_tk, 500 + 36), (12500, 16), jnp.float32)
        tbl_37 = 0.05 * jax.random.normal(jax.random.fold_in(_tk, 500 + 37), (12500, 16), jnp.float32)
        tbl_38 = 0.05 * jax.random.normal(jax.random.fold_in(_tk, 500 + 38), (12500, 16), jnp.float32)
        _rk = jax.random.fold_in(_tk, 7)
        W_top1 = 0.0606339 * jax.random.normal(jax.random.fold_in(_tk, 801), (272, 512), jnp.float32)
        W_top2 = 0.0441942 * jax.random.normal(jax.random.fold_in(_tk, 802), (512, 256), jnp.float32)
        W_top3 = 0.0625 * jax.random.normal(jax.random.fold_in(_tk, 803), (256, 1), jnp.float32)
        b_top1 = jnp.zeros((512,), jnp.float32)
        b_top2 = jnp.zeros((256,), jnp.float32)
        return (dense_ctx, ids, tbl_0, tbl_1, tbl_2, tbl_3, tbl_4, tbl_5, tbl_6, tbl_7, tbl_8, tbl_9, tbl_10, tbl_11, tbl_12, tbl_13, tbl_14, tbl_15, tbl_16, tbl_17, tbl_18, tbl_19, tbl_20, tbl_21, tbl_22, tbl_23, tbl_24, tbl_25, tbl_26, tbl_27, tbl_28, tbl_29, tbl_30, tbl_31, tbl_32, tbl_33, tbl_34, tbl_35, tbl_36, tbl_37, tbl_38, W_top1, b_top1, W_top2, b_top2, W_top3)
    dense_ctx, ids, tbl_0, tbl_1, tbl_2, tbl_3, tbl_4, tbl_5, tbl_6, tbl_7, tbl_8, tbl_9, tbl_10, tbl_11, tbl_12, tbl_13, tbl_14, tbl_15, tbl_16, tbl_17, tbl_18, tbl_19, tbl_20, tbl_21, tbl_22, tbl_23, tbl_24, tbl_25, tbl_26, tbl_27, tbl_28, tbl_29, tbl_30, tbl_31, tbl_32, tbl_33, tbl_34, tbl_35, tbl_36, tbl_37, tbl_38, W_top1, b_top1, W_top2, b_top2, W_top3 = _rec_inputs()

    def _L0_rec_setup():
        import jax, jax.numpy as jnp
        import numpy as np
        B, F0, D = (256, 39, 16)
        H1, H2 = (128, 128)
        key = jax.random.key(seed)
        k1, k2, k3 = jax.random.split(key, 3)
        x = jax.random.normal(k1, (B, F0, D), dtype=jnp.float32)

        def xavier(k, out_c, in_c):
            bound = np.sqrt(6.0 / (in_c + out_c)).astype(np.float32)
            return jax.random.uniform(k, (out_c, in_c, 1), dtype=jnp.float32, minval=-bound, maxval=bound)
        W0 = xavier(k2, H1, F0 * F0)
        W1 = xavier(k3, H2, F0 * H1)
        return {'input': x, 'W0': W0, 'W1': W1}
    _L0_rec_all = _L0_rec_setup()
    _L0_rec_in = {k: v for k, v in _L0_rec_all.items() if k in ('W0', 'W1')}
    del _L0_rec_all
    return {'dense_ctx': dense_ctx, 'ids': ids, 'tbl_0': tbl_0, 'tbl_1': tbl_1, 'tbl_2': tbl_2, 'tbl_3': tbl_3, 'tbl_4': tbl_4, 'tbl_5': tbl_5, 'tbl_6': tbl_6, 'tbl_7': tbl_7, 'tbl_8': tbl_8, 'tbl_9': tbl_9, 'tbl_10': tbl_10, 'tbl_11': tbl_11, 'tbl_12': tbl_12, 'tbl_13': tbl_13, 'tbl_14': tbl_14, 'tbl_15': tbl_15, 'tbl_16': tbl_16, 'tbl_17': tbl_17, 'tbl_18': tbl_18, 'tbl_19': tbl_19, 'tbl_20': tbl_20, 'tbl_21': tbl_21, 'tbl_22': tbl_22, 'tbl_23': tbl_23, 'tbl_24': tbl_24, 'tbl_25': tbl_25, 'tbl_26': tbl_26, 'tbl_27': tbl_27, 'tbl_28': tbl_28, 'tbl_29': tbl_29, 'tbl_30': tbl_30, 'tbl_31': tbl_31, 'tbl_32': tbl_32, 'tbl_33': tbl_33, 'tbl_34': tbl_34, 'tbl_35': tbl_35, 'tbl_36': tbl_36, 'tbl_37': tbl_37, 'tbl_38': tbl_38, 'W_top1': W_top1, 'b_top1': b_top1, 'W_top2': W_top2, 'b_top2': b_top2, 'W_top3': W_top3, 'L0_rec_W0': _L0_rec_in['W0'], 'L0_rec_W1': _L0_rec_in['W1']}

def reference(dense_ctx, ids, tbl_0, tbl_1, tbl_2, tbl_3, tbl_4, tbl_5, tbl_6, tbl_7, tbl_8, tbl_9, tbl_10, tbl_11, tbl_12, tbl_13, tbl_14, tbl_15, tbl_16, tbl_17, tbl_18, tbl_19, tbl_20, tbl_21, tbl_22, tbl_23, tbl_24, tbl_25, tbl_26, tbl_27, tbl_28, tbl_29, tbl_30, tbl_31, tbl_32, tbl_33, tbl_34, tbl_35, tbl_36, tbl_37, tbl_38, W_top1, b_top1, W_top2, b_top2, W_top3, L0_rec_W0, L0_rec_W1):
    import jax
    import jax.numpy as jnp

    def _L0_rec_ref(input, W0, W1):
        import jax, jax.numpy as jnp
        import numpy as np
        B, F0, D = (256, 39, 16)
        H1, H2 = (128, 128)
        x0 = input
        h = input
        outs = []
        for W in (W0, W1):
            Hout, P, _ = W.shape
            Hk = h.shape[1]
            Wr = W[:, :, 0].reshape(Hout, x0.shape[1], Hk)
            h = jnp.einsum('bfd,bqd,hfq->bhd', x0, h, Wr)
            outs.append(h)
        result = jnp.concatenate(outs, axis=1)
        return jnp.sum(result, axis=2)
    e = jnp.stack([tbl_0[ids[:, 0]], tbl_1[ids[:, 1]], tbl_2[ids[:, 2]], tbl_3[ids[:, 3]], tbl_4[ids[:, 4]], tbl_5[ids[:, 5]], tbl_6[ids[:, 6]], tbl_7[ids[:, 7]], tbl_8[ids[:, 8]], tbl_9[ids[:, 9]], tbl_10[ids[:, 10]], tbl_11[ids[:, 11]], tbl_12[ids[:, 12]], tbl_13[ids[:, 13]], tbl_14[ids[:, 14]], tbl_15[ids[:, 15]], tbl_16[ids[:, 16]], tbl_17[ids[:, 17]], tbl_18[ids[:, 18]], tbl_19[ids[:, 19]], tbl_20[ids[:, 20]], tbl_21[ids[:, 21]], tbl_22[ids[:, 22]], tbl_23[ids[:, 23]], tbl_24[ids[:, 24]], tbl_25[ids[:, 25]], tbl_26[ids[:, 26]], tbl_27[ids[:, 27]], tbl_28[ids[:, 28]], tbl_29[ids[:, 29]], tbl_30[ids[:, 30]], tbl_31[ids[:, 31]], tbl_32[ids[:, 32]], tbl_33[ids[:, 33]], tbl_34[ids[:, 34]], tbl_35[ids[:, 35]], tbl_36[ids[:, 36]], tbl_37[ids[:, 37]], tbl_38[ids[:, 38]]], axis=1)
    z = _L0_rec_ref(e, L0_rec_W0, L0_rec_W1)
    z = z.reshape(z.shape[0], -1)
    h = jnp.concatenate([z, dense_ctx], axis=1)
    h = jnp.maximum(h @ W_top1 + b_top1, 0.0)
    h = jnp.maximum(h @ W_top2 + b_top2, 0.0)
    y = h @ W_top3
    return y

_drawn_inputs = setup_inputs


def setup_inputs(seed=0):
    import zlib

    import numpy as np

    out = dict(_drawn_inputs(seed))
    spreads = {'b_top1': (0.0, 0.1), 'b_top2': (0.0, 0.1)}
    factors = {'tbl_0': 6.641,
     'tbl_1': 6.34,
     'tbl_2': 6.893,
     'tbl_3': 6.857,
     'tbl_4': 7.257,
     'tbl_5': 7.176,
     'tbl_6': 6.815,
     'tbl_7': 7.072,
     'tbl_8': 6.913,
     'tbl_9': 7.085,
     'tbl_10': 6.973,
     'tbl_11': 6.672,
     'tbl_12': 7.015,
     'tbl_13': 6.955,
     'tbl_14': 7.268,
     'tbl_15': 7.173,
     'tbl_16': 6.615,
     'tbl_17': 7.451,
     'tbl_18': 6.894,
     'tbl_19': 7.239,
     'tbl_20': 6.546,
     'tbl_21': 7.065,
     'tbl_22': 7.355,
     'tbl_23': 6.946,
     'tbl_24': 6.472,
     'tbl_25': 7.007,
     'tbl_26': 6.952,
     'tbl_27': 6.769,
     'tbl_28': 6.687,
     'tbl_29': 6.914,
     'tbl_30': 6.694,
     'tbl_31': 6.679,
     'tbl_32': 7.103,
     'tbl_33': 6.924,
     'tbl_34': 6.857,
     'tbl_35': 6.628,
     'tbl_36': 7.485,
     'tbl_37': 6.427,
     'tbl_38': 6.954,
     'L0_rec_W1': 8.0}
    for name, (base, spread) in spreads.items():
        noise = np.random.default_rng([zlib.crc32(name.encode()), seed]).standard_normal(out[name].shape)
        drawn = base * np.exp(spread * noise) if base else spread * noise
        out[name] = jnp.asarray(drawn.astype(out[name].dtype))
    for name, factor in factors.items():
        out[name] = (out[name] * factor).astype(out[name].dtype)
    return out
```

```python
import numpy as np
import concourse.bass as bass
from concourse import mybir
from contextlib import ExitStack

F32 = mybir.dt.float32
F32R = mybir.dt.float32r
BF16 = mybir.dt.bfloat16
I32 = mybir.dt.int32
ALU = mybir.AluOpType
ACT = mybir.ActivationFunctionType

P = 128
F = 39
D = 16
B = 2048
NT = B // P
HID = 128
DG = 4
CH = D // DG
NCOL = DG * P
NB = 8
NG = P // NB
FX = F + 1
FULL = 6
PT = FULL + 1
REST = 12
HH, LH, HL = 0, 32, 64
RROWS = HL + REST
SLOTS = CH * PT
L1_LAG = 4
ZL_LAG = 2
NZ = 4
NSPLIT = 3 * F
TOP1, TOP2 = 512, 256
DENSE = 16
BC = 512
XT_A, X1_A, XT_B, X1_B = 24, 25, 26, 27
HT0, G0 = 5, 9
L2_SLOTS, L2_PER = 8, 5


def pair_tables():
    base = list(range(REST))
    left = [-1] * P
    for start in (HH, LH, HL):
        left[start:start + REST] = base
    others = [f for f in range(REST, F) for _ in range(3)] + list(range(REST, REST + P - 3 * F))
    for r in range(P):
        if left[r] < 0:
            left[r] = others.pop(0)
    room = [FULL * left.count(f) + (1 if f < REST else 0) for f in range(F)]
    held = [[] for _ in range(F)]

    def move(pair, f, seen):
        seen.add(f)
        if len(held[f]) < room[f]:
            held[f].append(pair)
            return True
        for n, other in enumerate(held[f]):
            if other[0] == other[1]:
                continue
            to = other[0] if other[1] == f else other[1]
            if to in seen:
                continue
            held[f][n] = pair
            if move(other, to, seen):
                return True
            held[f][n] = other
        return False

    for i in range(F):
        for j in range(i, F):
            assert move((i, j), i, set()) or move((i, j), j, set())
    right = [[-1] * P for _ in range(PT)]

    def second(f):
        i, j = held[f].pop(0)
        return j if i == f else i

    for n, f in enumerate(base):
        for start in (HH, LH, HL):
            right[FULL][start + n] = held[f][0][0] if held[f][0][1] == f else held[f][0][1]
        held[f].pop(0)
    for t in range(FULL):
        for r in range(P):
            right[t][r] = second(left[r])
    return left, right


def at_least(engine, semaphore, value):
    if not isinstance(value, int) or value > 0:
        engine.wait_ge(semaphore, value)


def dlrm(nc, ids, tables, sel, ident, mask, w0a, w0b, w1t, wt1, b1, wt2, b2, wt3, denset, y):
    ctx = ExitStack()
    with ctx:
        def sb(name, shape, dt=F32):
            return ctx.enter_context(nc.sbuf_tensor(name, shape, dt))

        def sem(name):
            return ctx.enter_context(nc.semaphore(name))

        idx = sb("idx", [P, 2, F], I32)
        X = sb("X", [P, 2, F * D])
        X3 = sb("X3", [P, D, 3, F], BF16)
        R1 = sb("R1", [P, D, F])
        XT = sb("XT", [NSPLIT, 2, P, D], BF16)
        LEFT = sb("LEFT", [P, 2, NCOL])
        Z = sb("Z", [P, NZ, NCOL])
        ZH = sb("ZH", [P, PT, NCOL], F32R)
        ZL = sb("ZL", [P, PT, NCOL], F32R)
        H = sb("H", [P, P, D])
        HT = sb("HT", [P, NG, HID])
        X1 = sb("X1", [P, NG, FX])
        XB = sb("XB", [P, NG, FX, NB])
        G = sb("G", [P, FX, P])
        W0H = sb("W0H", [P, PT, HID], F32R)
        W0L = sb("W0L", [P, PT, HID], F32R)
        W1 = sb("W1", [P, F, HID])
        WT1 = sb("WT1", [P, 2, TOP1])
        WT1D = sb("WT1D", [DENSE, TOP1])
        WT2 = sb("WT2", [P, TOP1 // P, TOP2])
        WT3 = sb("WT3", [P, TOP2 // P])
        B1 = sb("B1", [P, TOP1 // P])
        B2 = sb("B2", [P, TOP2 // P])
        ZT = sb("ZT", [P, 2, B])
        DT = sb("DT", [DENSE, B])
        SEL = sb("SEL", [NSPLIT, PT + 1, P], BF16)
        SELX = sb("SELX", [NSPLIT, FX], BF16)
        IDF = sb("IDF", [P, P])
        IDB = sb("IDB", [P, P], BF16)
        MASK = sb("MASK", [P, NB])
        YS = sb("YS", [1, B])
        SELF = G[0:NSPLIT, 0:PT + 2, :]
        W0A = XB[:, 0:3, :, :].rearrange("p g f b -> p (g f b)")[:, 0:PT * HID]
        W0B = XB[:, 3:6, :, :].rearrange("p g f b -> p (g f b)")[:, 0:PT * HID]
        M1 = ctx.enter_context(nc.sbuf_tensor("M1", [P, TOP1 // P, BC], F32))
        M2 = ctx.enter_context(nc.sbuf_tensor("M2", [P, TOP2 // P, BC], F32))

        bank = [ctx.enter_context(nc.psum_tensor(f"bank{n}", [P, NCOL], F32)) for n in range(8)]
        ring = bank[0:4]
        acc = bank[4:6]
        turn = bank[6]
        turnb = turn[:, :].bitcast(BF16)
        gl = bank[7]

        s_in = sem("constants_loaded")
        s_w = sem("weights_loaded")
        s_cst = sem("constants_ready")
        s_w0s = sem("w0_summed")
        s_w0h = sem("w0_high_ready")
        s_w0l = sem("w0_ready")
        idx_ready = [sem(f"idx_ready{s}") for s in range(2)]
        gathered = [sem(f"gathered{s}") for s in range(2)]
        gathers_begun = sem("gathers_begun")
        part_h, part_r, part_m, part_l = sem("part_h"), sem("part_r"), sem("part_m"), sem("part_l")
        xt_filled, xt_drained = sem("xt_filled"), sem("xt_drained")
        x1_filled, x1_drained = sem("x1_filled"), sem("x1_drained")
        ht_filled, ht_drained = sem("ht_filled"), sem("ht_drained")
        left_filled, left_drained = sem("left_filled"), sem("left_drained")
        right_filled = sem("right_filled")
        z_done, zh_done, zl_done, z_used = sem("z_done"), sem("zh_done"), sem("zl_done"), sem("z_used")
        h_filled, h_drained = sem("h_filled"), sem("h_drained")
        xb_done = sem("xb_done")
        g_filled, g_drained = sem("g_filled"), sem("g_drained")
        l2_filled, l2_drained = sem("l2_filled"), sem("l2_drained")
        out1_done = sem("out1_done")
        m_filled, m_drained = sem("mlp_filled"), sem("mlp_drained")
        s_y = sem("y_stored")

        NCONST = 3

        def walk(engine, tile):
            for n in (0, 1):
                tile(n, n // 2, n)
            with engine.Fori(1, NT // 2 - 1) as i:
                for n in (2, 3):
                    tile(2 * i + n % 2, i, n)
            for n in (NT - 2, NT - 1, NT, NT + 1):
                tile(n, n // 2, n)

        def rows(j):
            return RROWS if j == FULL else P

        def buffer_free(engine, chunk, j):
            if j == FULL:
                at_least(engine, h_filled, chunk)
            else:
                at_least(engine, z_used, FULL * chunk - FULL + j + 1)

        block = ctx.enter_context(nc.Block())

        @block.sync
        def _(sp):
            ids_v = ids.rearrange("(t p) f -> t p f", p=P)
            for s in range(2):
                sp.dma_start(idx[:, s, :], ids_v[s, :, :]).then_inc(idx_ready[s], 16)
            sp.dma_start(SELF, sel.rearrange("p (t m) -> p t m", m=P)).then_inc(s_in, 16)
            sp.dma_start(IDF[:, :], ident).then_inc(s_in, 16)
            sp.dma_start(MASK[:, :], mask).then_inc(s_in, 16)
            sp.dma_start(W0A, w0a).then_inc(s_w, 16)
            sp.dma_start(W0B, w0b).then_inc(s_w, 16)
            sp.dma_start(W1[:, :, :], w1t.rearrange("q (f h) -> q f h", h=HID)).then_inc(s_w, 16)
            sp.dma_start(WT1[:, :, :], wt1[0:2 * P, :].rearrange("(t p) m -> p t m", p=P)).then_inc(s_w, 16)
            sp.dma_start(WT1D[:, :], wt1[2 * P:2 * P + DENSE, :]).then_inc(s_w, 16)
            sp.dma_start(WT2[:, :, :], wt2.rearrange("(t p) m -> p t m", p=P)).then_inc(s_w, 16)
            sp.dma_start(WT3[:, :], wt3).then_inc(s_w, 16)
            sp.dma_start(B1[:, :], b1).then_inc(s_w, 16)
            sp.dma_start(B2[:, :], b2).then_inc(s_w, 16)
            sp.dma_start(DT[:, :], denset).then_inc(s_w, 16)
            with sp.Fori(1, NT // 2) as i:
                for s in range(2):
                    sp.wait_ge(gathered[s], i * (16 * F))
                    sp.dma_start(idx[:, s, :], ids_v[bass.ds(2 * i + s, 1), :, :]
                                 .rearrange("o p f -> (o p) f")).then_inc(idx_ready[s], 16)
            for c in range(B // BC):
                sp.wait_ge(m_drained, 7 * (c + 1))
                sp.dma_start(y[:, c * BC:(c + 1) * BC], YS[0:1, c * BC:(c + 1) * BC]).then_inc(s_y, 16)
            sp.wait_ge(s_y, 16 * (B // BC))

        @block.gpsimd
        def _(pool):
            def gather(s):
                for f in range(F):
                    nc.gpsimd.indirect_dma_start(
                        out=X[:, s, f * D:(f + 1) * D], out_offset=None, in_=tables[f],
                        in_offset=bass.IndirectOffsetOnAxis(ap=idx[:, s, f:f + 1], axis=0),
                    ).then_inc(gathered[s], 16)

            for s in range(2):
                pool.wait_ge(idx_ready[s], 16)
                gather(s)
            with pool.Fori(1, NT // 2) as i:
                for s in range(2):
                    pool.wait_ge(idx_ready[s], 16 * i + 16)
                    pool.wait_ge(part_r, 2 * i + s - 1)
                    pool.sem_inc(gathers_begun, 1)
                    gather(s)

        @block.scalar
        def _(act):
            A = nc.scalar.activation
            act.wait_ge(s_in, 16 * NCONST)
            A(SEL[:, :, :], SELF[:, 0:PT + 1, :], ACT.Copy).then_inc(s_cst, 1)
            A(SELX[:, :], SELF[:, PT + 1, 0:FX], ACT.Copy).then_inc(s_cst, 1)
            A(IDB[:, :], IDF[:, :], ACT.Copy).then_inc(s_cst, 1)

            def first_part(t, half, n):
                act.wait_ge(gathered[n % 2], half * (16 * F) + 16 * F)
                at_least(act, xt_filled, 2 * t)
                A(X3[:, :, 0, :], X[:, n % 2, :].rearrange("p (f d) -> p d f", d=D), ACT.Copy).then_inc(part_h, 1)

            def second_part(t, n):
                act.wait_ge(part_r, t + 1)
                A(X3[:, :, 1, :], R1[:, :, :], ACT.Copy).then_inc(part_m, 1)

            def drain_xt(t, n, part):
                act.wait_ge(xt_filled, 2 * t + part + 1)
                A(XT[:, n % 2, :, 8 * part:8 * part + 8],
                  turnb[0:NSPLIT, :].rearrange("p (d b) -> p b d", b=P), ACT.Copy).then_inc(xt_drained, 1)

            def drain_left(c, m):
                act.wait_ge(left_filled, c + 1)
                A(LEFT[:, m % 2, :], ring[1][:, :], ACT.Copy).then_inc(left_drained, 1)

            def tile(t, half, n):
                for k in range(SLOTS):
                    c, j = k // PT, k % PT
                    item = SLOTS * t + k
                    if n < NT:
                        if j == 5 and (c < CH - 1 or n < NT - 1):
                            drain_left(CH * t + c + 1, c + 1)
                        act.wait_ge(z_done, item + 1)
                        buffer_free(act, CH * t + c, j)
                        A(ZH[0:rows(j), k % PT, :], Z[0:rows(j), k % NZ, :], ACT.Copy).then_inc(zh_done, 1)
                    for cc in range(CH):
                        if (PT * cc + PT - 1 + L1_LAG + 1) % SLOTS == k:
                            own = PT * cc + PT - 1 + L1_LAG + 1 < SLOTS
                            if (n < NT) if own else (1 <= n <= NT):
                                chunk = CH * (t if own else t - 1) + cc
                                act.wait_ge(h_filled, chunk + 1)
                                A(H[:, :, DG * cc:DG * cc + DG], acc[cc % 2][:, :].rearrange("p (b d) -> p b d", d=DG),
                                  ACT.Copy).then_inc(h_drained, 1)
                    if 1 <= n <= NT:
                        if k < NB:
                            if k == 0:
                                act.wait_ge(x1_drained, 2 * t)
                            A(XB[:, :, 0:F, k], X1[:, :, 0:F], ACT.Copy, scale=MASK[:, k:k + 1]).then_inc(xb_done, 1)
                        if HT0 <= k < HT0 + 4:
                            q = k - HT0
                            act.wait_ge(ht_filled, 4 * (t - 1) + q + 1)
                            A(HT[:, 4 * q:4 * q + 4, :], turn[:, :].rearrange("p (g h) -> p g h", h=HID),
                              ACT.Copy).then_inc(ht_drained, 1)
                    if 2 <= n and k == 0:
                        act.wait_ge(g_drained, NG * (t - 1))
                        A(ZT[:, 0, bass.ds((t - 2) * P, P)], G[:, F, :], ACT.Copy).then_inc(out1_done, 1)
                    if 2 <= n and k == L2_SLOTS:
                        act.wait_ge(l2_filled, t - 1)
                        act.wait_ge(out1_done, t - 1)
                        A(ZT[:, 1, bass.ds((t - 2) * P, P)], gl[:, 0:P], ACT.Copy).then_inc(l2_drained, 1)
                    if 1 <= n <= NT and G0 <= k < G0 + NG:
                        g = k - G0
                        act.wait_ge(g_filled, NG * (t - 1) + g + 1)
                        A(G[:, :, NB * g:NB * g + NB], gl[:, 0:FX * NB].rearrange("p (f b) -> p f b", b=NB),
                          ACT.Copy).then_inc(g_drained, 1)
                    if n < NT - 1:
                        if k == 21:
                            first_part(t + 1, half + n % 2, n + 1)
                        if k == 22:
                            second_part(t + 1, n + 1)
                        if k in (XT_A, XT_B):
                            drain_xt(t + 1, n + 1, int(k == XT_B))
                    if n < NT and k in (X1_A, X1_B):
                        part = int(k == X1_B)
                        act.wait_ge(x1_filled, 2 * t + part + 1)
                        if part == 0:
                            at_least(act, xb_done, NB * t)
                        A(X1[:, 8 * part:8 * part + 8, :], turn[:, 0:8 * FX].rearrange("p (g f) -> p g f", f=FX),
                          ACT.Copy).then_inc(x1_drained, 1)

            first_part(0, 0, 0)
            second_part(0, 0)
            act.wait_ge(s_w0s, 1)
            A(W0H[:, :, :], W0A.rearrange("p (t h) -> p t h", h=HID), ACT.Copy).then_inc(s_w0h, 1)
            drain_xt(0, 0, 0)
            drain_xt(0, 0, 1)
            drain_left(0, 0)
            act.wait_ge(s_w0l, 2)
            for g in range(NG):
                A(XB[:, g, F, :], MASK[:, :], ACT.Copy).then_inc(s_w0h, 1)
            walk(act, tile)
            u = 0
            for c in range(B // BC):
                for m in range(TOP1 // P):
                    u += 1
                    act.wait_ge(m_filled, u)
                    A(M1[:, m, :], bank[(u - 1) % 4][:, :], ACT.Relu, bias=B1[:, m:m + 1]).then_inc(m_drained, 1)
                for m in range(TOP2 // P):
                    u += 1
                    act.wait_ge(m_filled, u)
                    A(M2[:, m, :], bank[(u - 1) % 4][:, :], ACT.Relu, bias=B2[:, m:m + 1]).then_inc(m_drained, 1)
                u += 1
                act.wait_ge(m_filled, u)
                A(YS[0:1, c * BC:(c + 1) * BC], bank[(u - 1) % 4][0:1, :], ACT.Copy).then_inc(m_drained, 1)

        @block.vector
        def _(dve):
            TT = nc.vector.tensor_tensor

            def remainders(t, n):
                dve.wait_ge(part_h, t + 1)
                TT(R1[:, :, :], X[:, n % 2, :].rearrange("p (f d) -> p d f", d=D), X3[:, :, 0, :],
                   ALU.subtract).then_inc(part_r, 1)

            def last_part(t, n):
                dve.wait_ge(part_m, t + 1)
                TT(X3[:, :, 2, :], R1[:, :, :], X3[:, :, 1, :], ALU.subtract).then_inc(part_l, 1)

            def low(t, k):
                item = SLOTS * t + k
                dve.wait_ge(zh_done, item + 1)
                s = k % PT
                buffer_free(dve, CH * t + k // PT, s)
                if k % PT == FULL:
                    r = slice(LH, LH + REST)
                    TT(ZH[r, s, :], Z[r, k % NZ, :], ZH[r, s, :].bitcast(F32), ALU.subtract).then_inc(zl_done, 1)
                else:
                    TT(ZL[:, s, :], Z[:, k % NZ, :], ZH[:, s, :].bitcast(F32), ALU.subtract).then_inc(zl_done, 1)

            remainders(0, 0)
            last_part(0, 0)
            dve.wait_ge(s_w, 160)
            TT(W0A, W0A, W0B, ALU.add).then_inc(s_w0s, 1)
            dve.wait_ge(s_w0h, 1)
            TT(W0L[:, :, :], W0A.rearrange("p (t h) -> p t h", h=HID), W0H[:, :, :].bitcast(F32),
               ALU.subtract).then_inc(s_w0l, 1)
            dve.wait_ge(s_w0l, 1)
            nc.vector.tensor_copy(W0H[HL:HL + REST, FULL, :], W0L[HL:HL + REST, FULL, :].bitcast(F32)).then_inc(s_w0l, 1)

            def tile(t, half, n):
                for k in range(SLOTS):
                    c, j = k // PT, k % PT
                    item = SLOTS * t + k
                    if n < NT:
                        if j == 0:
                            dve.wait_ge(left_drained, CH * t + c + 1)
                        dve.wait_ge(right_filled, item + 1)
                        at_least(dve, zl_done, item + 1 - NZ)
                        TT(Z[0:rows(j), k % NZ, :], LEFT[0:rows(j), c % 2, :], ring[BANK[j]][0:rows(j), :],
                           ALU.mult).then_inc(z_done, 1)
                    if n < NT and k >= ZL_LAG:
                        low(t, k - ZL_LAG)
                    if 1 <= n <= NT and k < ZL_LAG:
                        low(t - 1, k - ZL_LAG + SLOTS)
                    if n < NT - 1:
                        if k == 21:
                            remainders(t + 1, n + 1)
                        if k == 22:
                            last_part(t + 1, n + 1)

            walk(dve, tile)

        @block.tensor
        def _(pe):
            MM = nc.tensor.matmul

            def turn_x(t, n, part):
                for d in range(8 * part, 8 * part + 8):
                    last = nc.tensor.transpose(turnb[0:NSPLIT, (d % 8) * P:(d % 8 + 1) * P],
                                               X3[:, d, :, :].rearrange("p s f -> p (s f)"), IDB[:, :])
                last.then_inc(xt_filled, 1)

            def select_left(c, cc, n):
                MM(ring[1][:, :], SEL[:, PT, :], XT[:, n % 2, :, DG * cc:DG * cc + DG],
                   start=True, stop=True).then_inc(left_filled, 1)

            def select_right(t, n, k):
                c, j = k // PT, k % PT
                MM(ring[BANK[j]][0:rows(j), :], SEL[:, j, 0:rows(j)],
                   XT[:, n % 2, :, DG * c:DG * c + DG],
                   start=True, stop=True).then_inc(right_filled, 1)

            def layer1(t, k):
                c, j = k // PT, k % PT
                s = k % PT
                pe.wait_ge(zl_done, SLOTS * t + k + 1)
                if j == 0:
                    at_least(pe, h_drained, CH * t + c - 1)
                out = acc[c % 2][:, :]
                if j == FULL:
                    MM(out, W0H[0:RROWS, j, :], ZH[0:RROWS, s, :], start=False, stop=True).then_inc(h_filled, 1)
                else:
                    MM(out, W0H[:, j, :], ZH[:, s, :], start=(j == 0), stop=False)
                    MM(out, W0H[:, j, :], ZL[:, s, :], start=False, stop=False)
                    MM(out, W0L[:, j, :], ZH[:, s, :], start=False, stop=False).then_inc(z_used, 1)

            pe.wait_ge(part_l, 1)
            pe.wait_ge(s_cst, 3)
            turn_x(0, 0, 0)
            pe.wait_ge(xt_drained, 1)
            turn_x(0, 0, 1)
            pe.wait_ge(xt_drained, 1)
            select_left(0, 0, 0)
            pe.wait_ge(s_w0l, 2)

            def tile(t, half, n):
                for k in range(SLOTS):
                    c, j = k // PT, k % PT
                    item = SLOTS * t + k
                    C = CH * t + c
                    if n < NT:
                        if j == 5 and (c < CH - 1 or n < NT - 1):
                            at_least(pe, z_done, PT * C + 2)
                            if c == 1:
                                pe.wait_ge(xt_drained, 2 * t + 2)
                            if c == CH - 1:
                                pe.wait_ge(xt_drained, 2 * t + 3)
                                select_left(C + 1, 0, n + 1)
                            else:
                                select_left(C + 1, c + 1, n)
                        if j == 1:
                            pe.wait_ge(left_drained, C + 1)
                        else:
                            at_least(pe, z_done, PT * C + FREE[j])
                        select_right(t, n, k)
                    if n < NT and k >= L1_LAG:
                        layer1(t, k - L1_LAG)
                    if 1 <= n <= NT and k < L1_LAG:
                        layer1(t - 1, k - L1_LAG + SLOTS)
                    if 2 <= n and k < L2_SLOTS:
                        if k == 0:
                            pe.wait_ge(g_drained, NG * (t - 1))
                        for f in range(L2_PER * k, min(L2_PER * k + L2_PER, F)):
                            last = MM(gl[:, 0:P], W1[:, f, :], G[:, f, :], start=(f == 0), stop=(f == F - 1))
                        if k == L2_SLOTS - 1:
                            last.then_inc(l2_filled, 1)
                    if 1 <= n <= NT and HT0 <= k < HT0 + 4:
                        q = k - HT0
                        if q == 0:
                            pe.wait_ge(h_drained, CH * t)
                            pe.wait_ge(x1_drained, 2 * t)
                        else:
                            pe.wait_ge(ht_drained, 4 * (t - 1) + q)
                        for g in range(4 * q, 4 * q + 4):
                            last = nc.tensor.transpose(turn[:, (g % 4) * HID:(g % 4 + 1) * HID],
                                                       H[:, NB * g:NB * g + NB, :].rearrange("p b d -> p (b d)"), IDF[:, :])
                        last.then_inc(ht_filled, 1)
                    if 1 <= n <= NT and G0 <= k < G0 + NG:
                        g = k - G0
                        if g % 4 == 0:
                            pe.wait_ge(ht_drained, 4 * (t - 1) + g // 4 + 1)
                        if g == 0:
                            pe.wait_ge(xb_done, NB * t)
                            pe.wait_ge(s_w0h, 1 + NG)
                            at_least(pe, l2_drained, t - 1)
                        else:
                            pe.wait_ge(g_drained, NG * (t - 1) + g)
                        MM(gl[:, 0:FX * NB], HT[:, g, :], XB[:, g, :, :].rearrange("p f b -> p (f b)"),
                           start=True, stop=True).then_inc(g_filled, 1)
                    if n < NT - 1 and k in (XT_A, XT_B):
                        if k == XT_A:
                            pe.wait_ge(part_l, t + 2)
                            if n > 0:
                                pe.wait_ge(ht_drained, 4 * t)
                            else:
                                pe.wait_ge(xt_drained, 2)
                        else:
                            pe.wait_ge(x1_drained, 2 * t + 1)
                        turn_x(t + 1, n + 1, int(k == XT_B))
                    if n < NT and k in (X1_A, X1_B):
                        part = int(k == X1_B)
                        if n < NT - 1:
                            pe.wait_ge(xt_drained, 2 * t + 3 + part)
                        elif part:
                            pe.wait_ge(x1_drained, 2 * t + 1)
                        else:
                            pe.wait_ge(ht_drained, 4 * t)
                        for g in range(8 * part, 8 * part + 8):
                            last = MM(turn[:, (g % 8) * FX:(g % 8 + 1) * FX], XT[:, n % 2, NB * g:NB * g + NB, :].rearrange("p b d -> p (b d)"),
                                      SELX[:, :], start=True, stop=True)
                        last.then_inc(x1_filled, 1)

            walk(pe, tile)
            pe.wait_ge(s_w, 160)
            pe.wait_ge(l2_drained, NT)
            u = 0
            for c in range(B // BC):
                cols = slice(c * BC, (c + 1) * BC)
                for m in range(TOP1 // P):
                    at_least(pe, m_drained, u - 3)
                    ms = slice(m * P, (m + 1) * P)
                    out = bank[u % 4][:, :]
                    MM(out, WT1[:, 0, ms], ZT[:, 0, cols], start=True, stop=False)
                    MM(out, WT1[:, 1, ms], ZT[:, 1, cols], start=False, stop=False)
                    MM(out, WT1D[:, ms], DT[:, cols], start=False, stop=True).then_inc(m_filled, 1)
                    u += 1
                for m in range(TOP2 // P):
                    pe.wait_ge(m_drained, 7 * c + 4)
                    ms = slice(m * P, (m + 1) * P)
                    for q in range(TOP1 // P):
                        last = MM(bank[u % 4][:, :], WT2[:, q, ms], M1[:, q, :], start=(q == 0), stop=(q == TOP1 // P - 1))
                    last.then_inc(m_filled, 1)
                    u += 1
                pe.wait_ge(m_drained, 7 * c + 6)
                for q in range(TOP2 // P):
                    last = MM(bank[u % 4][0:1, :], WT3[:, q:q + 1], M2[:, q, :], start=(q == 0), stop=(q == 1))
                last.then_inc(m_filled, 1)
                u += 1


BANK = [0, 1, 2, 3, 0, 2, 3]
FREE = [-2, 0, -1, 0, 1, 3, 4]


def kernel(**inputs):
    import concourse.bacc as bacc
    from concourse.bass_utils import run_bass_kernel_spmd

    left, right = pair_tables()
    arrays = {}

    def lay(name, a):
        arrays[name] = np.ascontiguousarray(a)

    lay("ids", inputs["ids"])
    for f in range(F):
        lay(f"tbl_{f}", inputs[f"tbl_{f}"])
    wanted = np.full((PT + 2, P), -1)
    wanted[:PT] = right
    wanted[PT] = left
    wanted[PT + 1, :F] = np.arange(F)
    sel = (np.arange(NSPLIT)[:, None, None] % F == wanted[None]).astype(np.float32)
    lay("sel", sel.reshape(NSPLIT, -1))
    lay("ident", np.eye(P, dtype=np.float32))
    lay("mask", (np.arange(P)[:, None] // D == np.arange(NB)[None]).astype(np.float32))
    w0 = np.asarray(inputs["L0_rec_W0"]).reshape(HID, F, F)
    pad = np.zeros((HID, F + 1, F + 1), w0.dtype)
    pad[:, :F, :F] = w0
    ll = np.broadcast_to(np.array(left), (PT, P))
    rr = np.array(right)
    li = np.where(rr < 0, F, ll)
    ri = np.where(rr < 0, F, rr)
    lay("w0a", pad[:, li, ri].transpose(2, 1, 0).reshape(P, -1))
    same = li == ri
    lay("w0b", pad[:, np.where(same, F, ri), np.where(same, F, li)].transpose(2, 1, 0).reshape(P, -1))
    lay("w1t", np.asarray(inputs["L0_rec_W1"]).reshape(HID, F, HID).transpose(2, 1, 0).reshape(HID, F * HID))
    lay("wt1", inputs["W_top1"])
    lay("wt2", inputs["W_top2"])
    lay("wt3", np.asarray(inputs["W_top3"]).reshape(TOP2 // P, P).T)
    lay("b1", np.asarray(inputs["b_top1"]).reshape(TOP1 // P, P).T)
    lay("b2", np.asarray(inputs["b_top2"]).reshape(TOP2 // P, P).T)
    lay("denset", np.asarray(inputs["dense_ctx"]).T)

    nc = bacc.Bacc("TRN2", target_bir_lowering=False, num_devices=1)
    ap = {k: nc.dram_tensor(k, a.shape, mybir.dt.from_np(a.dtype), kind="ExternalInput").ap()
          for k, a in arrays.items()}
    y = nc.dram_tensor("y", (1, B), F32, kind="ExternalOutput").ap()
    dlrm(nc, ap["ids"], [ap[f"tbl_{f}"] for f in range(F)], ap["sel"], ap["ident"], ap["mask"],
         ap["w0a"], ap["w0b"], ap["w1t"], ap["wt1"], ap["b1"], ap["wt2"], ap["b2"], ap["wt3"], ap["denset"], y)
    out = run_bass_kernel_spmd(nc, [arrays], core_ids=[0]).results[0]["y"]
    return out.reshape(B, 1)
```

```python
L2D=1; OUT1=22
ASKEW=0; DSKEW=0
import numpy as np
import concourse.bass as bass
from concourse import mybir
from contextlib import ExitStack

F32 = mybir.dt.float32
F32R = mybir.dt.float32r
BF16 = mybir.dt.bfloat16
I32 = mybir.dt.int32
ALU = mybir.AluOpType
ACT = mybir.ActivationFunctionType

P = 128
F = 39
D = 16
B = 2048
NT = B // P
HID = 128
DG = 4
CH = D // DG
NCOL = DG * P
NB = 8
NG = P // NB
FX = F + 1
FULL = 6
PT = FULL + 1
REST = 12
HH, LH, HL = 0, 32, 64
RROWS = HL + REST
SLOTS = CH * PT
L1_LAG = 4
ZL_LAG = 1
NZ = 4
UNITS = 7
NSPLIT = 3 * F
TOP1, TOP2 = 512, 256
DENSE = 16
BC = 512
XT_A, X1_A, XT_B, X1_B = 22,23,25,26
HT_AT = (5, 6, 7, 8)
G_AT = (9, 10, 11, 11, 12, 13, 14, 15, 15, 16, 17, 18, 19, 19, 20, 21)
L2_AT = (22, 23, 24, 25, 26, 27, 28, 29, 30, 31)
SPLIT = 19
MLP0=9
MLP_IN=8
MLP_AT=[MLP0+(27-MLP0)*u//20 for u in range(21)]
DROWS = HL + DENSE


def pair_tables():
    base = list(range(REST))
    left = [-1] * P
    for start in (HH, LH, HL):
        left[start:start + REST] = base
    others = [f for f in range(REST, F) for _ in range(3)] + list(range(REST, REST + P - 3 * F))
    for r in range(P):
        if left[r] < 0:
            left[r] = others.pop(0)
    room = [FULL * left.count(f) + (1 if f < REST else 0) for f in range(F)]
    held = [[] for _ in range(F)]

    def move(pair, f, seen):
        seen.add(f)
        if len(held[f]) < room[f]:
            held[f].append(pair)
            return True
        for n, other in enumerate(held[f]):
            if other[0] == other[1]:
                continue
            to = other[0] if other[1] == f else other[1]
            if to in seen:
                continue
            held[f][n] = pair
            if move(other, to, seen):
                return True
            held[f][n] = other
        return False

    for i in range(F):
        for j in range(i, F):
            assert move((i, j), i, set()) or move((i, j), j, set())
    right = [[-1] * P for _ in range(PT)]

    def second(f):
        i, j = held[f].pop(0)
        return j if i == f else i

    for n, f in enumerate(base):
        for start in (HH, LH, HL):
            right[FULL][start + n] = held[f][0][0] if held[f][0][1] == f else held[f][0][1]
        held[f].pop(0)
    for t in range(FULL):
        for r in range(P):
            right[t][r] = second(left[r])
    return left, right


def at_least(engine, semaphore, value):
    if not isinstance(value, int) or value > 0:
        engine.wait_ge(semaphore, value)


def dlrm(nc, ids, tables, sel, ident, w0a, w0b, w1t, wt1, b1, wt2, b2, wt3, denset, y):
    ctx = ExitStack()
    with ctx:
        def sb(name, shape, dt=F32):
            return ctx.enter_context(nc.sbuf_tensor(name, shape, dt))

        def sem(name):
            return ctx.enter_context(nc.semaphore(name))

        idx = sb("idx", [P, 2, F], I32)
        X = sb("X", [P, 2, F * D])
        X3 = sb("X3", [P, D, 3, F], BF16)
        XT = sb("XT", [NSPLIT, 2, P, D], BF16)
        LEFT = sb("LEFT", [P, 2, NCOL])
        Z = sb("Z", [P, NZ, NCOL])
        ZH = sb("ZH", [P, PT, NCOL], F32R)
        ZL = sb("ZL", [P, PT, NCOL], F32R)
        H = sb("H", [P, P, D])
        HTH = sb("HTH", [P, NG, HID], F32R)
        HTL = sb("HTL", [P, NG, HID], F32R)
        X1H = sb("X1H", [P, NG, FX], F32R)
        X1L = sb("X1L", [P, NG, FX], F32R)
        XBH = sb("XBH", [P, NB, NG, FX], F32R)
        XBL = sb("XBL", [P, NB, NG, FX], F32R)
        G = sb("G", [P, FX, P])
        W0H = sb("W0H", [P, PT + 1, HID], F32R)
        W0L = sb("W0L", [P, PT + 1, HID], F32R)
        W1 = sb("W1", [P, F, HID])
        WT1 = sb("WT1", [P, 2, TOP1])
        WTD = sb("WTD", [DROWS, TOP1], F32R)
        WT2H = sb("WT2H", [P, TOP1 // P, TOP2], F32R)
        WT2L = sb("WT2L", [P, TOP1 // P, TOP2], F32R)
        WT3 = sb("WT3", [P, TOP2 // P])
        B1 = sb("B1", [P, TOP1 // P])
        B2 = sb("B2", [P, TOP2 // P])
        ZT = sb("ZT", [P, 2, B])
        SEL = sb("SEL", [NSPLIT, PT + 1, P], BF16)
        SELX = sb("SELX", [NSPLIT, FX], BF16)
        IDF = sb("IDF", [P, P])
        IDB = sb("IDB", [P, P], BF16)
        SELF = G[0:NSPLIT, 0:PT + 2, :]
        W0S = G[:, 10:10 + 2 * PT, :].rearrange("p (o t) h -> p o t h", o=2)
        WT2S = Z[:, 2:4, :].rearrange("p a (b m) -> p (a b) m", m=TOP2)
        WTDS = LEFT[0:DROWS, 0, :]
        ZTH, ZTL = ZH[:, 4:6, :], ZL[:, 4:6, :]
        M1H, M1L = ZH[:, 0:4, :], ZL[:, 0:4, :]
        M1 = Z[:, 2:4, :]
        M2 = Z[:, 0:2, :]
        DT = X1H[0:DROWS, :, :].rearrange("p g f -> p (g f)")[:, 0:BC]
        WT1H = W0H[:, :, :].rearrange("p (q a) h -> p q (a h)", q=2)
        WT1L = W0L[:, :, :].rearrange("p (q a) h -> p q (a h)", q=2)
        YS = X[0:1, 0, 0:BC]

        bank = [ctx.enter_context(nc.psum_tensor(f"bank{n}", [P, NCOL], F32)) for n in range(8)]
        ring = bank[0:4]
        acc = bank[4:6]
        turn = bank[6]
        turnb = turn[:, :].bitcast(BF16)
        gl = bank[7]
        two = (turn, gl)

        s_in = sem("constants_loaded")
        s_w = sem("weights_loaded")
        s_cst = sem("constants_ready")
        s_zero = sem("buffers_zeroed")
        s_top = sem("mlp_high_ready")
        s_topl = sem("mlp_weights_ready")
        s_dense = [sem(f"dense_loaded{s}") for s in range(2)]
        zt_high, zt_low = sem("mlp_input_high"), sem("mlp_input_low")
        m_high, m_low = sem("mlp_hidden_high"), sem("mlp_hidden_low")
        x1_low, ht_low = sem("x1_low_done"), sem("ht_low_done")
        s_w0s = sem("w0_summed")
        s_w0h = sem("w0_high_ready")
        s_w0l = sem("w0_ready")
        idx_ready = [sem(f"idx_ready{s}") for s in range(2)]
        gathered = [sem(f"gathered{s}") for s in range(2)]
        gathers_begun = sem("gathers_begun")
        part_h, part_r, part_m, part_l = sem("part_h"), sem("part_r"), sem("part_m"), sem("part_l")
        xt_filled, xt_drained = sem("xt_filled"), sem("xt_drained")
        x1_filled, x1_drained = sem("x1_filled"), sem("x1_drained")
        ht_filled, ht_drained = sem("ht_filled"), sem("ht_drained")
        left_filled, left_drained = sem("left_filled"), sem("left_drained")
        right_filled = sem("right_filled")
        z_done, zh_done, zl_done, z_used = sem("z_done"), sem("zh_done"), sem("zl_done"), sem("z_used")
        h_filled, h_drained = sem("h_filled"), sem("h_drained")
        xb_done = sem("xb_done")
        g_filled, g_drained = sem("g_filled"), sem("g_drained")
        l2_filled, l2_drained = sem("l2_filled"), sem("l2_drained")
        out1_done = sem("out1_done")
        m_filled, m_drained = sem("mlp_filled"), sem("mlp_drained")
        s_y = sem("y_stored")

        NCONST, NWEIGHT = 2, 11

        def walk(engine, tile):
            for n in (0, 1):
                tile(n, n // 2, n)
            with engine.Fori(1, NT // 2 - 1) as i:
                for n in (2, 3):
                    tile(2 * i + n % 2, i, n)
            for n in (NT - 2, NT - 1, NT, NT + 1):
                tile(n, n // 2, n)

        def rows(j):
            return RROWS if j == FULL else P

        def buffer_free(engine, chunk, j):
            if j == FULL:
                at_least(engine, h_filled, chunk)
            else:
                at_least(engine, z_used, FULL * chunk - FULL + j + 1)

        block = ctx.enter_context(nc.Block())

        @block.sync
        def _(sp):
            ids_v = ids.rearrange("(t p) f -> t p f", p=P)
            for s in range(2):
                sp.dma_start(idx[:, s, :], ids_v[s, :, :]).then_inc(idx_ready[s], 16)
            sp.dma_start(SELF, sel.rearrange("p (t m) -> p t m", m=P)).then_inc(s_in, 16)
            sp.dma_start(IDF[:, :], ident).then_inc(s_in, 16)
            for o, w in enumerate((w0a, w0b)):
                sp.dma_start(W0S[:, o, :, :], w.rearrange("p (t h) -> p t h", h=HID)).then_inc(s_w, 16)
            sp.dma_start(W1[:, :, :], w1t.rearrange("q (f h) -> q f h", h=HID)).then_inc(s_w, 16)
            sp.dma_start(WT1[:, :, :], wt1[0:2 * P, :].rearrange("(t p) m -> p t m", p=P)).then_inc(s_w, 16)
            sp.dma_start(WT2S, wt2.rearrange("(t p) m -> p t m", p=P)).then_inc(s_w, 16)
            sp.wait_ge(s_zero, 1)
            for r in (HH, LH, HL):
                sp.dma_start(WTDS[r:r + DENSE, :], wt1[2 * P:2 * P + DENSE, :]).then_inc(s_w, 16)
            sp.dma_start(WT3[:, :], wt3).then_inc(s_w, 16)
            sp.dma_start(B1[:, :], b1).then_inc(s_w, 16)
            sp.dma_start(B2[:, :], b2).then_inc(s_w, 16)

            def spread(t):
                sp.wait_ge(x1_low, 2 * t + 2)
                for XB, X1 in ((XBH, X1H), (XBL, X1L)):
                    for b in range(NB):
                        sp.dma_start(XB[D * b:D * b + D, b, :, :].bitcast(F32),
                                     X1[D * b:D * b + D, :, :].bitcast(F32)).then_inc(xb_done, 16)

            sp.wait_ge(s_zero, 5)
            def store(c):
                sp.wait_ge(m_drained, UNITS * (c + 1))
                sp.dma_start(y[:, c * BC:(c + 1) * BC], YS).then_inc(s_y, 16)

            with sp.Fori(0, NT // 2 - 1) as i:
                for s in range(2):
                    sp.wait_ge(gathered[s], i * (16 * F) + 16 * F)
                    sp.dma_start(idx[:, s, :], ids_v[bass.ds(2 * i + s + 2, 1), :, :]
                                 .rearrange("o p f -> (o p) f")).then_inc(idx_ready[s], 16)
                    spread(2 * i + s)
            for t in (NT - 2, NT - 1):
                spread(t)
            for c in range(B // BC):
                if c < 2:
                    sp.wait_ge(z_done, SLOTS * NT - PT * (1 - c))
                else:
                    sp.wait_ge(zt_low, 2 * c - 2)
                for r in (HH, LH, HL):
                    sp.dma_start(LEFT[r:r + DENSE, c % 2, :], denset[:, c * BC:(c + 1) * BC]).then_inc(s_dense[c % 2], 16)
                if c >= 1:
                    store(c - 1)
            store(B // BC - 1)
            sp.wait_ge(s_y, 16 * (B // BC))

        @block.gpsimd
        def _(pool):
            def gather(s):
                for f in range(F):
                    nc.gpsimd.indirect_dma_start(
                        out=X[:, s, f * D:(f + 1) * D], out_offset=None, in_=tables[f],
                        in_offset=bass.IndirectOffsetOnAxis(ap=idx[:, s, f:f + 1], axis=0),
                    ).then_inc(gathered[s], 16)

            for s in range(2):
                pool.wait_ge(idx_ready[s], 16)
                gather(s)
            with pool.Fori(1, NT // 2) as i:
                for s in range(2):
                    pool.wait_ge(idx_ready[s], 16 * i + 16)
                    pool.wait_ge(part_l, 2 * i + s - 1)
                    pool.sem_inc(gathers_begun, 1)
                    gather(s)

        @block.scalar
        def _(act):
            A = nc.scalar.activation

            def first_part(t, half, n):
                act.wait_ge(gathered[n % 2], half * (16 * F) + 16 * F)
                at_least(act, xt_filled, 2 * t)
                A(X3[:, :, 0, :], X[:, n % 2, :].rearrange("p (f d) -> p d f", d=D), ACT.Copy).then_inc(part_h, 1)

            def second_part(t, n):
                act.wait_ge(part_r, t + 1)
                A(X3[:, :, 1, :], X[:, n % 2, :].rearrange("p (f d) -> p d f", d=D), ACT.Copy).then_inc(part_m, 1)

            def drain_xt(t, n, part):
                act.wait_ge(xt_filled, 2 * t + part + 1)
                A(XT[:, n % 2, :, 8 * part:8 * part + 8],
                  turnb[0:NSPLIT, :].rearrange("p (d b) -> p b d", b=P), ACT.Copy).then_inc(xt_drained, 1)

            def drain_left(chunk, cc):
                act.wait_ge(left_filled, chunk + 1)
                A(LEFT[:, cc % 2, :], ring[1][:, :], ACT.Copy).then_inc(left_drained, 1)

            def drain_h(t, cc):
                act.wait_ge(h_filled, CH * t + cc + 1)
                A(H[:, :, DG * cc:DG * cc + DG], acc[cc % 2][:, :].rearrange("p (b d) -> p b d", d=DG),
                  ACT.Copy).then_inc(h_drained, 1)

            def high_ht(t, q):
                act.wait_ge(ht_filled, 4 * t + q + 1)
                A(HTH[:, 4 * q:4 * q + 4, :], two[q % 2][:, :].rearrange("p (g h) -> p g h", h=HID), ACT.Copy).then_inc(ht_drained, 1)

            def drain_g(t, g):
                act.wait_ge(g_filled, NG * t + g + 1)
                A(G[:, :, NB * g:NB * g + NB], two[g % 2][:, 0:FX * NB].rearrange("p (b f) -> p f b", b=NB),
                  ACT.Copy).then_inc(g_drained, 1)

            def high_x1(t, part):
                act.wait_ge(x1_filled, 2 * t + part + 1)
                at_least(act, xb_done, 16 * 2 * NB * t)
                A(X1H[:, 8 * part:8 * part + 8, 0:F],
                  turn[:, 0:8 * FX].rearrange("p (g f) -> p g f", f=FX)[:, :, 0:F], ACT.Copy).then_inc(x1_drained, 1)

            def mlp_input(c):
                if c >= 1:
                    act.wait_ge(m_filled, UNITS * (c - 1) + 4)
                act.wait_ge(out1_done, 4 * c + 4)
                act.wait_ge(l2_drained, 4 * c + 4)
                if c == 0:
                    A(WT1H, WT1[:, :, :], ACT.Copy).then_inc(s_top, 1)
                A(ZTH, ZT[:, :, c * BC:(c + 1) * BC], ACT.Copy).then_inc(zt_high, 1)
                act.wait_ge(s_dense[c % 2], 48 * (c // 2 + 1))
                if c == 0:
                    act.wait_ge(xb_done, 16 * 2 * NB * NT)
                A(DT, LEFT[0:DROWS, c % 2, :], ACT.Copy).then_inc(zt_high, 1)

            def mlp(u):
                c, m = u // UNITS, u % UNITS
                act.wait_ge(m_filled, u + 1)
                out = bank[u % 4][:, :]
                if m < 4:
                    at_least(act, m_low, 4 * c + m - 1)
                    A(M1[:, m % 2, :], out, ACT.Relu, bias=B1[:, m:m + 1]).then_inc(m_drained, 1)
                    act.wait_ge(m_drained, u + 1)
                    A(M1H[:, m, :], M1[:, m % 2, :], ACT.Copy).then_inc(m_high, 1)
                elif m < 6:
                    A(M2[:, m - 4, :], out, ACT.Relu, bias=B2[:, m - 4:m - 3]).then_inc(m_drained, 1)
                else:
                    at_least(act, s_y, 16 * c)
                    A(YS, out[0:1, :], ACT.Copy).then_inc(m_drained, 1)
                if m == 4 and c < B // BC - 2:
                    mlp_input(c + 1)

            def tile(t, half, n):
                for k in range(SLOTS):
                    c, j = k // PT, k % PT
                    was = k + ASKEW
                    if 1 <= n <= NT:
                        for g in range(NG):
                            if G_AT[g] == was:
                                drain_g(t - 1, g)
                    if n < NT and j == 5 and (c < CH - 1 or n < NT - 1):
                        drain_left(CH * t + c + 1, c + 1)
                    if 2 <= n and was == L2_AT[-1] - SLOTS + L2D:
                        act.wait_ge(l2_filled, t - 1)
                        A(ZT[:, 1, bass.ds((t - 2) * P, P)], gl[:, 0:P], ACT.Copy).then_inc(l2_drained, 1)
                    if 1 <= n <= NT:
                        if k == L1_LAG:
                            drain_h(t - 1, CH - 1)
                        if was in HT_AT:
                            high_ht(t - 1, HT_AT.index(was))
                    if n < NT:
                        for cc in range(CH - 1):
                            if k == PT * (cc + 1) + L1_LAG:
                                drain_h(t, cc)
                        if was in (X1_A, X1_B):
                            high_x1(t, int(was == X1_B))
                    if n < NT - 1:
                        if k == SPLIT:
                            first_part(t + 1, half + n % 2, n + 1)
                        if k == SPLIT + 1:
                            second_part(t + 1, n + 1)
                        if was in (XT_A, XT_B):
                            drain_xt(t + 1, n + 1, int(was == XT_B))
                    if 1 <= n <= NT and k == OUT1:
                        act.wait_ge(g_drained, NG * t)
                        A(ZT[:, 0, bass.ds((t - 1) * P, P)], G[:, F, :], ACT.Copy).then_inc(out1_done, 1)
                    if n < NT:
                        act.wait_ge(z_done, SLOTS * t + k + 1)
                        buffer_free(act, CH * t + c, j)
                        A(ZH[0:rows(j), j, :], Z[0:rows(j), k % NZ, :], ACT.Copy).then_inc(zh_done, 1)
                    if n == NT and k == MLP_IN:
                        mlp_input(0)
                    for u, at in enumerate(MLP_AT):
                        if n == NT and at == was:
                            mlp(u)

            act.wait_ge(s_in, 16 * NCONST)
            A(SEL[:, :, :], SELF[:, 0:PT + 1, :], ACT.Copy).then_inc(s_cst, 1)
            A(SELX[:, :], SELF[:, PT + 1, 0:FX], ACT.Copy).then_inc(s_cst, 1)
            A(IDB[:, :], IDF[:, :], ACT.Copy).then_inc(s_cst, 1)
            act.wait_ge(s_w, 16 * NWEIGHT)
            A(WT2H[:, :, :], WT2S, ACT.Copy).then_inc(s_top, 1)
            A(WTD[:, :], WTDS, ACT.Copy).then_inc(s_top, 1)
            act.wait_ge(s_w0s, 1)
            A(W0H[:, 0:PT, :], W0S[:, 0, :, :], ACT.Copy).then_inc(s_w0h, 1)
            first_part(0, 0, 0)
            second_part(0, 0)
            drain_xt(0, 0, 0)
            drain_xt(0, 0, 1)
            act.wait_ge(s_topl, 2)
            drain_left(0, 0)
            walk(act, tile)
            mlp_input(B // BC - 1)
            for u in range(3 * UNITS, 4 * UNITS):
                mlp(u)

        @block.vector
        def _(dve):
            TT = nc.vector.tensor_tensor

            def first_rest(t, n):
                dve.wait_ge(part_h, t + 1)
                x = X[:, n % 2, :].rearrange("p (f d) -> p d f", d=D)
                TT(x, x, X3[:, :, 0, :], ALU.subtract).then_inc(part_r, 1)

            def last_part(t, n):
                dve.wait_ge(part_m, t + 1)
                TT(X3[:, :, 2, :], X[:, n % 2, :].rearrange("p (f d) -> p d f", d=D), X3[:, :, 1, :],
                   ALU.subtract).then_inc(part_l, 1)

            def low(t, k):
                j = k % PT
                dve.wait_ge(zh_done, SLOTS * t + k + 1)
                buffer_free(dve, CH * t + k // PT, j)
                if j == FULL:
                    r = slice(LH, LH + REST)
                    TT(ZH[r, j, :], Z[r, k % NZ, :], ZH[r, j, :].bitcast(F32), ALU.subtract).then_inc(zl_done, 1)
                else:
                    TT(ZL[:, j, :], Z[:, k % NZ, :], ZH[:, j, :].bitcast(F32), ALU.subtract).then_inc(zl_done, 1)

            def low_ht(t, q):
                dve.wait_ge(ht_drained, 4 * t + q + 1)
                TT(HTL[:, 4 * q:4 * q + 4, :], two[q % 2][:, :].rearrange("p (g h) -> p g h", h=HID),
                   HTH[:, 4 * q:4 * q + 4, :].bitcast(F32), ALU.subtract).then_inc(ht_low, 1)

            def low_x1(t, part):
                dve.wait_ge(x1_drained, 2 * t + part + 1)
                gs = slice(8 * part, 8 * part + 8)
                TT(X1L[:, gs, 0:F], turn[:, 0:8 * FX].rearrange("p (g f) -> p g f", f=FX)[:, :, 0:F],
                   X1H[:, gs, 0:F].bitcast(F32), ALU.subtract).then_inc(x1_low, 1)

            def mlp_input(c):
                if c == 0:
                    dve.wait_ge(h_filled, CH * NT)
                    dve.wait_ge(s_top, 3)
                    TT(WT1L, WT1[:, :, :], WT1H.bitcast(F32), ALU.subtract).then_inc(s_topl, 1)
                dve.wait_ge(zt_high, 2 * c + 1)
                TT(ZTL, ZT[:, :, c * BC:(c + 1) * BC], ZTH.bitcast(F32), ALU.subtract).then_inc(zt_low, 1)
                dve.wait_ge(zt_high, 2 * c + 2)
                r = slice(LH, LH + DENSE)
                TT(DT[r, :], LEFT[r, c % 2, :], DT[r, :].bitcast(F32), ALU.subtract).then_inc(zt_low, 1)

            def mlp(u):
                c, m = u // UNITS, u % UNITS
                if m < 4:
                    dve.wait_ge(m_high, 4 * c + m + 1)
                    TT(M1L[:, m, :], M1[:, m % 2, :], M1H[:, m, :].bitcast(F32), ALU.subtract).then_inc(m_low, 1)
                if m == 4 and c < B // BC - 2:
                    mlp_input(c + 1)

            def tile(t, half, n):
                for k in range(SLOTS):
                    c, j = k // PT, k % PT
                    was = k + DSKEW
                    if n < NT:
                        if j == 0:
                            dve.wait_ge(left_drained, CH * t + c + 1)
                        dve.wait_ge(right_filled, SLOTS * t + k + 1)
                        at_least(dve, zl_done, SLOTS * t + k + 1 - NZ)
                        TT(Z[0:rows(j), k % NZ, :], LEFT[0:rows(j), c % 2, :], ring[BANK[j]][0:rows(j), :],
                           ALU.mult).then_inc(z_done, 1)
                    if 1 <= n <= NT and was in HT_AT:
                        low_ht(t - 1, HT_AT.index(was))
                    if n < NT and was in (X1_A, X1_B):
                        low_x1(t, int(was == X1_B))
                    if n < NT and k >= ZL_LAG:
                        low(t, k - ZL_LAG)
                    if 1 <= n <= NT and k < ZL_LAG:
                        low(t - 1, k - ZL_LAG + SLOTS)
                    if n < NT - 1:
                        if k == SPLIT:
                            first_rest(t + 1, n + 1)
                        if k == SPLIT + 1:
                            last_part(t + 1, n + 1)
                    if n == NT and k == MLP_IN:
                        mlp_input(0)
                    for u, at in enumerate(MLP_AT):
                        if n == NT and at == was:
                            mlp(u)

            nc.vector.memset(WTDS, 0.0).then_inc(s_zero, 1)
            nc.vector.memset(XBH[:, :, :, :].bitcast(F32), 0.0).then_inc(s_zero, 1)
            nc.vector.memset(XBL[:, :, :, :].bitcast(F32), 0.0).then_inc(s_zero, 1)
            nc.vector.memset(X1H[:, :, F:FX].bitcast(F32), 1.0).then_inc(s_zero, 1)
            nc.vector.memset(X1L[:, :, F:FX].bitcast(F32), 0.0).then_inc(s_zero, 1)
            dve.wait_ge(s_w, 16 * NWEIGHT)
            TT(W0S[:, 0, :, :], W0S[:, 0, :, :], W0S[:, 1, :, :], ALU.add).then_inc(s_w0s, 1)
            dve.wait_ge(s_top, 2)
            TT(WT2L[:, :, :], WT2S, WT2H[:, :, :].bitcast(F32), ALU.subtract).then_inc(s_topl, 1)
            r = slice(HL, HL + DENSE)
            TT(WTD[r, :], WTDS[r, :], WTD[r, :].bitcast(F32), ALU.subtract).then_inc(s_topl, 1)
            dve.wait_ge(s_w0h, 1)
            TT(W0L[:, 0:PT, :], W0S[:, 0, :, :], W0H[:, 0:PT, :].bitcast(F32), ALU.subtract).then_inc(s_w0l, 1)
            dve.wait_ge(s_w0l, 1)
            r = slice(HL, HL + REST)
            nc.vector.tensor_copy(W0H[r, FULL, :], W0L[r, FULL, :].bitcast(F32)).then_inc(s_w0l, 1)
            first_rest(0, 0)
            last_part(0, 0)
            walk(dve, tile)
            mlp_input(B // BC - 1)
            for u in range(3 * UNITS, 4 * UNITS):
                mlp(u)

        @block.tensor
        def _(pe):
            MM = nc.tensor.matmul

            def turn_x(t, n, part):
                for d in range(8 * part, 8 * part + 8):
                    last = nc.tensor.transpose(turnb[0:NSPLIT, (d % 8) * P:(d % 8 + 1) * P],
                                               X3[:, d, :, :].rearrange("p s f -> p (s f)"), IDB[:, :])
                last.then_inc(xt_filled, 1)

            def select_left(c, cc, n):
                MM(ring[1][:, :], SEL[:, PT, :], XT[:, n % 2, :, DG * cc:DG * cc + DG],
                   start=True, stop=True).then_inc(left_filled, 1)

            def select_right(t, n, k):
                c, j = k // PT, k % PT
                MM(ring[BANK[j]][0:rows(j), :], SEL[:, j, 0:rows(j)],
                   XT[:, n % 2, :, DG * c:DG * c + DG],
                   start=True, stop=True).then_inc(right_filled, 1)

            def layer1(t, k):
                c, j = k // PT, k % PT
                s = k % PT
                pe.wait_ge(zl_done, SLOTS * t + k + 1)
                if j == 0:
                    at_least(pe, h_drained, CH * t + c - 1)
                out = acc[c % 2][:, :]
                if j == FULL:
                    MM(out, W0H[0:RROWS, j, :], ZH[0:RROWS, s, :], start=False, stop=True).then_inc(h_filled, 1)
                else:
                    MM(out, W0H[:, j, :], ZH[:, s, :], start=(j == 0), stop=False)
                    MM(out, W0H[:, j, :], ZL[:, s, :], start=False, stop=False)
                    MM(out, W0L[:, j, :], ZH[:, s, :], start=False, stop=False).then_inc(z_used, 1)

            pe.wait_ge(part_l, 1)
            pe.wait_ge(s_cst, 3)
            turn_x(0, 0, 0)
            pe.wait_ge(xt_drained, 1)
            turn_x(0, 0, 1)
            pe.wait_ge(xt_drained, 1)
            select_left(0, 0, 0)
            pe.wait_ge(s_w0l, 2)
            pe.wait_ge(s_w, 16 * NWEIGHT)

            def mlp(u):
                c, m = u // UNITS, u % UNITS
                cols = slice(c * BC, (c + 1) * BC)
                at_least(pe, m_drained, u - 3)
                out = bank[u % 4][:, :]
                if m < 4:
                    ms = slice(m * P, (m + 1) * P)
                    if m == 0:
                        pe.wait_ge(s_topl, 3)
                        pe.wait_ge(zt_low, 2 * c + 2)
                    for q in range(2):
                        MM(out, WT1H[:, q, ms], ZTH[:, q, :], start=(q == 0), stop=False)
                        MM(out, WT1H[:, q, ms], ZTL[:, q, :], start=False, stop=False)
                        MM(out, WT1L[:, q, ms], ZTH[:, q, :], start=False, stop=False)
                    MM(out, WTD[:, ms], DT, start=False, stop=True).then_inc(m_filled, 1)
                elif m < 6:
                    ms = slice((m - 4) * P, (m - 3) * P)
                    for q in range(TOP1 // P):
                        if m == 4:
                            pe.wait_ge(m_low, 4 * c + q + 1)
                        MM(out, WT2H[:, q, ms], M1H[:, q, :], start=(q == 0), stop=False)
                        MM(out, WT2H[:, q, ms], M1L[:, q, :], start=False, stop=False)
                        last = MM(out, WT2L[:, q, ms], M1H[:, q, :], start=False, stop=(q == TOP1 // P - 1))
                    last.then_inc(m_filled, 1)
                else:
                    pe.wait_ge(m_drained, UNITS * c + 6)
                    for q in range(TOP2 // P):
                        last = MM(out[0:1, :], WT3[:, q:q + 1], M2[:, q, :], start=(q == 0), stop=(q == 1))
                    last.then_inc(m_filled, 1)

            def tile(t, half, n):
                for k in range(SLOTS):
                    c, j = k // PT, k % PT
                    item = SLOTS * t + k
                    C = CH * t + c
                    if n < NT:
                        if j == 5 and (c < CH - 1 or n < NT - 1):
                            at_least(pe, z_done, PT * C + 2)
                            if c == 1:
                                pe.wait_ge(xt_drained, 2 * t + 2)
                            if c == CH - 1:
                                pe.wait_ge(xt_drained, 2 * t + 3)
                                select_left(C + 1, 0, n + 1)
                            else:
                                select_left(C + 1, c + 1, n)
                        if j == 1:
                            pe.wait_ge(left_drained, C + 1)
                        else:
                            at_least(pe, z_done, PT * C + FREE[j])
                        select_right(t, n, k)
                    if n < NT and k >= L1_LAG:
                        layer1(t, k - L1_LAG)
                    if 1 <= n <= NT and k < L1_LAG:
                        layer1(t - 1, k - L1_LAG + SLOTS)
                    for m, at in enumerate(L2_AT):
                        if (1 <= n <= NT and at == k) or (2 <= n and at == k + SLOTS):
                            if m == 0:
                                pe.wait_ge(g_drained, NG * t)
                            n0, n1 = F * m // len(L2_AT), F * (m + 1) // len(L2_AT)
                            for f in range(n0, n1):
                                last = MM(gl[:, 0:P], W1[:, f, :], G[:, f, :], start=(f == 0), stop=(f == F - 1))
                            if n1 == F:
                                last.then_inc(l2_filled, 1)
                    if 1 <= n <= NT and k in HT_AT:
                        q = HT_AT.index(k)
                        if q == 0:
                            pe.wait_ge(h_drained, CH * t)
                            pe.wait_ge(x1_low, 2 * t)
                        elif q == 1:
                            at_least(pe, l2_drained, t - 1)
                        else:
                            pe.wait_ge(ht_low, 4 * (t - 1) + q - 1)
                        for g in range(4 * q, 4 * q + 4):
                            last = nc.tensor.transpose(two[q % 2][:, (g % 4) * HID:(g % 4 + 1) * HID],
                                                       H[:, NB * g:NB * g + NB, :].rearrange("p b d -> p (b d)"), IDF[:, :])
                        last.then_inc(ht_filled, 1)
                    for g in range(NG):
                        if not (1 <= n <= NT and G_AT[g] == k):
                            continue
                        if g % 4 == 0:
                            pe.wait_ge(ht_low, 4 * (t - 1) + g // 4 + 1)
                        if g == 0:
                            pe.wait_ge(xb_done, 16 * 2 * NB * t)
                            pe.wait_ge(ht_low, 4 * t - 1)
                        elif g == 1:
                            pe.wait_ge(ht_low, 4 * t)
                        else:
                            pe.wait_ge(g_drained, NG * (t - 1) + g - 1)
                        out = two[g % 2][:, 0:FX * NB]
                        MM(out, HTH[:, g, :], XBH[:, :, g, :], start=True, stop=False)
                        MM(out, HTH[:, g, :], XBL[:, :, g, :], start=False, stop=False)
                        MM(out, HTL[:, g, :], XBH[:, :, g, :], start=False, stop=True).then_inc(g_filled, 1)
                    if n < NT - 1 and k in (XT_A, XT_B):
                        if k == XT_A:
                            pe.wait_ge(part_l, t + 2)
                            if n > 0:
                                pe.wait_ge(g_drained, NG * t - 1)
                            else:
                                pe.wait_ge(xt_drained, 2)
                        else:
                            pe.wait_ge(x1_low, 2 * t + 1)
                        turn_x(t + 1, n + 1, int(k == XT_B))
                    if n < NT and k in (X1_A, X1_B):
                        part = int(k == X1_B)
                        if n < NT - 1:
                            pe.wait_ge(xt_drained, 2 * t + 3 + part)
                        elif part:
                            pe.wait_ge(x1_low, 2 * t + 1)
                        else:
                            pe.wait_ge(g_drained, NG * t - 1)
                        for g in range(8 * part, 8 * part + 8):
                            last = MM(turn[:, (g % 8) * FX:(g % 8 + 1) * FX], XT[:, n % 2, NB * g:NB * g + NB, :].rearrange("p b d -> p (b d)"),
                                      SELX[:, :], start=True, stop=True)
                        last.then_inc(x1_filled, 1)
                    for u, at in enumerate(MLP_AT):
                        if n == NT and at == k:
                            if u == 0:
                                pe.wait_ge(z_done, SLOTS * NT)
                            mlp(u)

            walk(pe, tile)
            for u in range(3 * UNITS, 4 * UNITS):
                mlp(u)


BANK = [0, 1, 2, 3, 0, 2, 3]
FREE = [-2, 0, -1, 0, 1, 3, 4]


def kernel(**inputs):
    import concourse.bacc as bacc
    from concourse.bass_utils import run_bass_kernel_spmd

    left, right = pair_tables()
    arrays = {}

    def lay(name, a):
        arrays[name] = np.ascontiguousarray(a)

    lay("ids", inputs["ids"])
    for f in range(F):
        lay(f"tbl_{f}", inputs[f"tbl_{f}"])
    wanted = np.full((PT + 2, P), -1)
    wanted[:PT] = right
    wanted[PT] = left
    wanted[PT + 1, :F] = np.arange(F)
    sel = (np.arange(NSPLIT)[:, None, None] % F == wanted[None]).astype(np.float32)
    lay("sel", sel.reshape(NSPLIT, -1))
    lay("ident", np.eye(P, dtype=np.float32))
    w0 = np.asarray(inputs["L0_rec_W0"]).reshape(HID, F, F)
    pad = np.zeros((HID, F + 1, F + 1), w0.dtype)
    pad[:, :F, :F] = w0
    ll = np.broadcast_to(np.array(left), (PT, P))
    rr = np.array(right)
    li = np.where(rr < 0, F, ll)
    ri = np.where(rr < 0, F, rr)
    lay("w0a", pad[:, li, ri].transpose(2, 1, 0).reshape(P, -1))
    same = li == ri
    lay("w0b", pad[:, np.where(same, F, ri), np.where(same, F, li)].transpose(2, 1, 0).reshape(P, -1))
    lay("w1t", np.asarray(inputs["L0_rec_W1"]).reshape(HID, F, HID).transpose(2, 1, 0).reshape(HID, F * HID))
    lay("wt1", inputs["W_top1"])
    lay("wt2", inputs["W_top2"])
    lay("wt3", np.asarray(inputs["W_top3"]).reshape(TOP2 // P, P).T)
    lay("b1", np.asarray(inputs["b_top1"]).reshape(TOP1 // P, P).T)
    lay("b2", np.asarray(inputs["b_top2"]).reshape(TOP2 // P, P).T)
    lay("denset", np.asarray(inputs["dense_ctx"]).T)

    nc = bacc.Bacc("TRN2", target_bir_lowering=False, num_devices=1)
    ap = {k: nc.dram_tensor(k, a.shape, mybir.dt.from_np(a.dtype), kind="ExternalInput").ap()
          for k, a in arrays.items()}
    y = nc.dram_tensor("y", (1, B), F32, kind="ExternalOutput").ap()
    dlrm(nc, ap["ids"], [ap[f"tbl_{f}"] for f in range(F)], ap["sel"], ap["ident"],
         ap["w0a"], ap["w0b"], ap["w1t"], ap["wt1"], ap["b1"], ap["wt2"], ap["b2"], ap["wt3"], ap["denset"], y)
    out = run_bass_kernel_spmd(nc, [arrays], core_ids=[0]).results[0]["y"]
    return out.reshape(B, 1)
```

```python
import numpy as np
import concourse.bass as bass
from concourse import mybir
from contextlib import ExitStack

F32 = mybir.dt.float32
F32R = mybir.dt.float32r
BF16 = mybir.dt.bfloat16
I32 = mybir.dt.int32
ALU = mybir.AluOpType
ACT = mybir.ActivationFunctionType

P = 128
F = 39
D = 16
B = 2048
NT = B // P
HID = 128
DG = 4
CH = D // DG
NCOL = DG * P
NB = 8
NG = P // NB
FX = F + 1
FULL = 6
PT = FULL + 1
REST = 12
HH, LH, HL = 0, 32, 64
RROWS = HL + REST
SLOTS = CH * PT
NZ = 6
UNITS = 7
NSPLIT = 3 * F
TOP1, TOP2 = 512, 256
DENSE = 16
BC = 512
DROWS = HL + DENSE

L1_LAG = 4
ZL_LAG = 1
ACT_LATE = 0
DVE_LATE = 1
SPLIT = 19
XT_A, XT_B = 22, 25
X1_A, X1_B = 23, 26
HT_AT = (5, 6, 7, 8)
G_AT = (10, 11, 12, 13, 14, 14, 15, 16, 16, 17, 18, 18, 19, 20, 20, 21)
OUT1_AT = 22
L2_AT = (22, 23, 24, 25, 26, 27, 28, 29, 30, 31, 32, 33)
L2_OUT = L2_AT[-1] - SLOTS + 1
MLP_IN = 4
MLP0 = 6
MLP_AT = [MLP0 + (SLOTS - 1 - MLP0) * u // (3 * UNITS - 1) for u in range(3 * UNITS)]


PICKED = (0, 2, 4, 6)
BANK = {0: 0, 2: 1, 4: 2, 6: 1}
FREE = {0: -6, 2: 0, 4: -2, 6: 3}
LEFT_BANK = 3
BUFFER = (0, 3, 1, 4, 0, 5, 2, 1, 3, 0, 4, 1, 5, 2)
AGO = (5, 7, 5, 7, 4, 7, 7, 5, 7, 5, 7, 4, 7, 7)
SHIFT = {1: 20, 3: 50, 5: 81}
NPICK = len(PICKED)
LEFT_AT = (3, 3, 3, 5)
LEFT_OF_ROW = [
    0, 1, 2, 3, 4, 5, 6, 7, 8, 9, 10, 11, 19, 12, 15, 20, 4, 36, 7, 33, 2, 10, 35, 0, 26, 18, 8, 23, 34, 22, 34, 6,
    0, 1, 2, 3, 4, 5, 6, 7, 8, 9, 10, 11, 14, 16, 27, 37, 31, 25, 32, 30, 30, 26, 19, 19, 21, 5, 1, 35, 36, 14, 32, 17,
    0, 1, 2, 3, 4, 5, 6, 7, 8, 9, 10, 11, 23, 16, 38, 21, 22, 16, 27, 24, 12, 3, 38, 17, 18, 13, 25, 20, 12, 37, 28, 38,
    27, 36, 13, 17, 24, 29, 21, 18, 26, 15, 28, 28, 25, 35, 20, 13, 37, 31, 23, 9, 14, 34, 29, 15, 24, 31, 33, 30, 22, 29, 32, 33,
]


def pair_tables():
    base = list(range(REST))
    left = LEFT_OF_ROW
    assert all(left[start:start + REST] == base for start in (HH, LH, HL))
    right = [[-1] * P for _ in range(PT)]
    for t, shift in SHIFT.items():
        right[t] = left[shift:] + left[:shift]
    moved = {(min(a, b), max(a, b)) for t in SHIFT for a, b in zip(left, right[t])}
    assert len(moved) == len(SHIFT) * P
    room = [len(PICKED[:-1]) * left.count(f) + (1 if f < REST else 0) for f in range(F)]
    held = [[] for _ in range(F)]

    def move(pair, f, seen):
        seen.add(f)
        if len(held[f]) < room[f]:
            held[f].append(pair)
            return True
        for n, other in enumerate(held[f]):
            if other[0] == other[1]:
                continue
            to = other[0] if other[1] == f else other[1]
            if to in seen:
                continue
            held[f][n] = pair
            if move(other, to, seen):
                return True
            held[f][n] = other
        return False

    for i in range(F):
        for j in range(i, F):
            if (i, j) not in moved:
                assert move((i, j), i, set()) or move((i, j), j, set())

    def second(f):
        i, j = held[f].pop(0)
        return j if i == f else i

    for n, f in enumerate(base):
        for start in (HH, LH, HL):
            right[FULL][start + n] = held[f][0][0] if held[f][0][1] == f else held[f][0][1]
        held[f].pop(0)
    for t in PICKED[:-1]:
        for r in range(P):
            right[t][r] = second(left[r])
    return left, right


def at_least(engine, semaphore, value):
    if not isinstance(value, int) or value > 0:
        engine.wait_ge(semaphore, value)


def dlrm(nc, ids, tables, sel, ident, w0a, w0b, w1t, wt1, b1, wt2, b2, wt3, denset, y):
    ctx = ExitStack()
    with ctx:
        def sb(name, shape, dt=F32):
            return ctx.enter_context(nc.sbuf_tensor(name, shape, dt))

        def sem(name):
            return ctx.enter_context(nc.semaphore(name))

        idx = sb("idx", [P, 2, F], I32)
        X = sb("X", [P, 2, F * D])
        X3 = sb("X3", [P, D, 3, F], BF16)
        XT = sb("XT", [NSPLIT, 2, P, D], BF16)
        LEFT = sb("LEFT", [P, 2, NCOL])
        Z = sb("Z", [P, NZ, NCOL])
        ZH = sb("ZH", [P, PT, NCOL], F32R)
        ZL = sb("ZL", [P, FULL, NCOL], F32R)
        H = sb("H", [P, P, D])
        HTH = sb("HTH", [P, NG, HID], F32R)
        HTL = sb("HTL", [P, NG, HID], F32R)
        X1 = sb("X1", [P, 2, NG, FX], F32R)
        XB = sb("XB", [P, 2, NB, NG, FX], F32R)
        G = sb("G", [P, FX, P])
        W0H = sb("W0H", [P, PT + 1, HID], F32R)
        W0L = sb("W0L", [P, PT + 1, HID], F32R)
        W1 = sb("W1", [P, F, HID])
        WT1 = sb("WT1", [P, 2, TOP1])
        WTD = sb("WTD", [DROWS, TOP1], F32R)
        WT2H = sb("WT2H", [P, TOP1 // P, TOP2], F32R)
        WT2L = sb("WT2L", [P, TOP1 // P, TOP2], F32R)
        WT3 = sb("WT3", [P, TOP2 // P])
        B1 = sb("B1", [P, TOP1 // P])
        B2 = sb("B2", [P, TOP2 // P])
        ZT = sb("ZT", [P, 2, B])
        SEL = sb("SEL", [NSPLIT, NPICK + 1, P], BF16)
        SELX = sb("SELX", [NSPLIT, FX], BF16)
        IDF = sb("IDF", [P, P])
        IDB = sb("IDB", [P, P], BF16)
        SELF = G[0:NSPLIT, 0:NPICK + 2, :]
        W0S = G[:, 10:10 + 2 * PT, :].rearrange("p (o t) h -> p o t h", o=2)
        WT2S = Z[:, 2:4, :].rearrange("p a (b m) -> p (a b) m", m=TOP2)
        WTDS = LEFT[0:DROWS, 0, :]
        ZTH, ZTL = ZH[:, 4:6, :], ZL[:, 4:6, :]
        M1H, M1L = ZH[:, 0:4, :], ZL[:, 0:4, :]
        M1 = Z[:, 2:4, :]
        M2 = Z[:, 0:2, :]
        DT = X1[0:DROWS, 0, :, :].rearrange("p g f -> p (g f)")[:, 0:BC]
        WT1H = W0H[:, :, :].rearrange("p (q a) h -> p q (a h)", q=2)
        WT1L = W0L[:, :, :].rearrange("p (q a) h -> p q (a h)", q=2)
        YS = X[0:1, 0, 0:BC]

        bank = [ctx.enter_context(nc.psum_tensor(f"bank{n}", [P, NCOL], F32)) for n in range(8)]
        ring = bank[0:4]
        acc = bank[4:6]
        turn = bank[6]
        turnb = turn[:, :].bitcast(BF16)
        gl = bank[7]
        two = (turn, gl)

        s_in = sem("constants_loaded")
        s_w = sem("weights_loaded")
        s_cst = sem("constants_ready")
        s_zero = sem("buffers_zeroed")
        s_top = sem("mlp_high_ready")
        s_topl = sem("mlp_weights_ready")
        s_dense = [sem(f"dense_loaded{s}") for s in range(2)]
        zt_high, zt_low = sem("mlp_input_high"), sem("mlp_input_low")
        m_high, m_low = sem("mlp_hidden_high"), sem("mlp_hidden_low")
        x1_low, ht_low = sem("x1_low_done"), sem("ht_low_done")
        s_w0s = sem("w0_summed")
        s_w0h = sem("w0_high_ready")
        s_w0l = sem("w0_ready")
        idx_ready = [sem(f"idx_ready{s}") for s in range(2)]
        gathered = [sem(f"gathered{s}") for s in range(2)]
        gathers_begun = sem("gathers_begun")
        part_h, part_r, part_m, part_l = sem("part_h"), sem("part_r"), sem("part_m"), sem("part_l")
        xt_filled, xt_drained = sem("xt_filled"), sem("xt_drained")
        x1_filled, x1_drained = sem("x1_filled"), sem("x1_drained")
        ht_filled, ht_drained = sem("ht_filled"), sem("ht_drained")
        left_filled, left_drained = sem("left_filled"), sem("left_drained")
        right_filled = sem("right_filled")
        moved = {j: sem(f"right_moved{j}") for j in SHIFT}
        z_done, zh_done, zl_done, z_used = sem("z_done"), sem("zh_done"), sem("zl_done"), sem("z_used")
        h_filled, h_drained = sem("h_filled"), sem("h_drained")
        xb_done = sem("xb_done")
        g_filled, g_drained = sem("g_filled"), sem("g_drained")
        moves_begun = sem("moves_begun")
        l2_filled, l2_drained = sem("l2_filled"), sem("l2_drained")
        out1_done = sem("out1_done")
        m_filled, m_drained = sem("mlp_filled"), sem("mlp_drained")
        s_y = sem("y_stored")

        NCONST, NWEIGHT = 2, 11

        def walk(engine, tile):
            for n in (0, 1):
                tile(n, n // 2, n)
            with engine.Fori(1, NT // 2 - 1) as i:
                for n in (2, 3):
                    tile(2 * i + n % 2, i, n)
            for n in (NT - 2, NT - 1, NT, NT + 1):
                tile(n, n // 2, n)

        def rows(j):
            return RROWS if j == FULL else P

        def buffer_free(engine, chunk, j):
            if j == FULL:
                at_least(engine, h_filled, chunk)
            else:
                at_least(engine, z_used, FULL * chunk - FULL + j + 1)

        block = ctx.enter_context(nc.Block())

        @block.sync
        def _(sp):
            ids_v = ids.rearrange("(t p) f -> t p f", p=P)
            for s in range(2):
                sp.dma_start(idx[:, s, :], ids_v[s, :, :]).then_inc(idx_ready[s], 16)
            sp.dma_start(SELF, sel.rearrange("p (t m) -> p t m", m=P)).then_inc(s_in, 16)
            sp.dma_start(IDF[:, :], ident).then_inc(s_in, 16)
            for o, w in enumerate((w0a, w0b)):
                sp.dma_start(W0S[:, o, :, :], w.rearrange("p (t h) -> p t h", h=HID)).then_inc(s_w, 16)
            sp.dma_start(W1[:, :, :], w1t.rearrange("q (f h) -> q f h", h=HID)).then_inc(s_w, 16)
            sp.dma_start(WT1[:, :, :], wt1[0:2 * P, :].rearrange("(t p) m -> p t m", p=P)).then_inc(s_w, 16)
            sp.dma_start(WT2S, wt2.rearrange("(t p) m -> p t m", p=P)).then_inc(s_w, 16)
            sp.wait_ge(s_zero, 1)
            for r in (HH, LH, HL):
                sp.dma_start(WTDS[r:r + DENSE, :], wt1[2 * P:2 * P + DENSE, :]).then_inc(s_w, 16)
            sp.dma_start(WT3[:, :], wt3).then_inc(s_w, 16)
            sp.dma_start(B1[:, :], b1).then_inc(s_w, 16)
            sp.dma_start(B2[:, :], b2).then_inc(s_w, 16)

            def spread(t, part):
                if part == 0:
                    sp.wait_ge(x1_low, 2 * t + 2)
                for b in range(NB // 2 * part, NB // 2 * (part + 1)):
                    sp.dma_start(XB[D * b:D * b + D, :, b, :, :].bitcast(F32),
                                 X1[D * b:D * b + D, :, :, :].bitcast(F32)).then_inc(xb_done, 16)

            def move(t, k):
                c, j = k // PT, k % PT
                if j == min(SHIFT):
                    sp.wait_ge(left_drained, CH * t + c + 1)
                    sp.sem_inc(moves_begun, 1)
                at_least(sp, zl_done, SLOTS * t + k + 1 - AGO[k % len(AGO)])
                up = SHIFT[j]
                sp.dma_start(Z[0:P - up, BUFFER[k % len(BUFFER)], :], LEFT[up:P, c % 2, :]).then_inc(moved[j], 16)
                sp.dma_start(Z[P - up:P, BUFFER[k % len(BUFFER)], :], LEFT[0:up, c % 2, :]).then_inc(moved[j], 16)

            def store(c):
                sp.wait_ge(m_drained, UNITS * (c + 1))
                sp.dma_start(y[:, c * BC:(c + 1) * BC], YS).then_inc(s_y, 16)

            def tile(t, half, n):
                for step, k in enumerate(k for k in range(SLOTS) if k % PT in SHIFT):
                    if n < NT:
                        move(t, k)
                    if n < NT - 2 and step == 4:
                        sp.wait_ge(gathered[n % 2], half * (16 * F) + 16 * F)
                        sp.dma_start(idx[:, n % 2, :], ids_v[bass.ds(t + 2, 1), :, :]
                                     .rearrange("o p f -> (o p) f")).then_inc(idx_ready[n % 2], 16)
                    if 1 <= n <= NT and step in (1, 2):
                        spread(t - 1, step - 1)

            sp.wait_ge(s_zero, 4)
            walk(sp, tile)
            for c in range(B // BC):
                if c < 2:
                    sp.wait_ge(z_done, SLOTS * NT - PT * (1 - c))
                else:
                    sp.wait_ge(zt_low, 2 * c - 2)
                for r in (HH, LH, HL):
                    sp.dma_start(LEFT[r:r + DENSE, c % 2, :], denset[:, c * BC:(c + 1) * BC]).then_inc(s_dense[c % 2], 16)
                if c >= 1:
                    store(c - 1)
            store(B // BC - 1)
            sp.wait_ge(s_y, 16 * (B // BC))

        @block.gpsimd
        def _(pool):
            def gather(s):
                for f in range(F):
                    nc.gpsimd.indirect_dma_start(
                        out=X[:, s, f * D:(f + 1) * D], out_offset=None, in_=tables[f],
                        in_offset=bass.IndirectOffsetOnAxis(ap=idx[:, s, f:f + 1], axis=0),
                    ).then_inc(gathered[s], 16)

            for s in range(2):
                pool.wait_ge(idx_ready[s], 16)
                gather(s)
            with pool.Fori(1, NT // 2) as i:
                for s in range(2):
                    pool.wait_ge(idx_ready[s], 16 * i + 16)
                    pool.wait_ge(part_l, 2 * i + s - 1)
                    pool.sem_inc(gathers_begun, 1)
                    gather(s)

        @block.scalar
        def _(act):
            A = nc.scalar.activation

            def first_part(t, half, n):
                act.wait_ge(gathered[n % 2], half * (16 * F) + 16 * F)
                at_least(act, xt_filled, 2 * t)
                A(X3[:, :, 0, :], X[:, n % 2, :].rearrange("p (f d) -> p d f", d=D), ACT.Copy).then_inc(part_h, 1)

            def second_part(t, n):
                act.wait_ge(part_r, t + 1)
                A(X3[:, :, 1, :], X[:, n % 2, :].rearrange("p (f d) -> p d f", d=D), ACT.Copy).then_inc(part_m, 1)

            def drain_xt(t, n, part):
                act.wait_ge(xt_filled, 2 * t + part + 1)
                A(XT[:, n % 2, :, 8 * part:8 * part + 8],
                  turnb[0:NSPLIT, :].rearrange("p (d b) -> p b d", b=P), ACT.Copy).then_inc(xt_drained, 1)

            def drain_left(chunk, cc):
                act.wait_ge(left_filled, chunk + 1)
                A(LEFT[:, cc % 2, :], ring[LEFT_BANK][:, :], ACT.Copy).then_inc(left_drained, 1)

            def drain_h(t, cc):
                act.wait_ge(h_filled, CH * t + cc + 1)
                A(H[:, :, DG * cc:DG * cc + DG], acc[cc % 2][:, :].rearrange("p (b d) -> p b d", d=DG),
                  ACT.Copy).then_inc(h_drained, 1)

            def high_ht(t, q):
                act.wait_ge(ht_filled, 4 * t + q + 1)
                A(HTH[:, 4 * q:4 * q + 4, :], two[q % 2][:, :].rearrange("p (g h) -> p g h", h=HID), ACT.Copy).then_inc(ht_drained, 1)

            def drain_g(t, g):
                act.wait_ge(g_filled, NG * t + g + 1)
                A(G[:, :, NB * g:NB * g + NB], two[g % 2][:, 0:FX * NB].rearrange("p (b f) -> p f b", b=NB),
                  ACT.Copy).then_inc(g_drained, 1)

            def high_x1(t, part):
                act.wait_ge(x1_filled, 2 * t + part + 1)
                at_least(act, xb_done, 16 * NB * t)
                A(X1[:, 0, 8 * part:8 * part + 8, 0:F],
                  turn[:, 0:8 * FX].rearrange("p (g f) -> p g f", f=FX)[:, :, 0:F], ACT.Copy).then_inc(x1_drained, 1)

            def mlp_input(c):
                if c >= 1:
                    act.wait_ge(m_filled, UNITS * (c - 1) + 4)
                act.wait_ge(out1_done, 4 * c + 4)
                act.wait_ge(l2_drained, 4 * c + 4)
                if c == 0:
                    act.wait_ge(h_drained, CH * NT)
                    A(WT1H, WT1[:, :, :], ACT.Copy).then_inc(s_top, 1)
                A(ZTH, ZT[:, :, c * BC:(c + 1) * BC], ACT.Copy).then_inc(zt_high, 1)
                act.wait_ge(s_dense[c % 2], 48 * (c // 2 + 1))
                if c == 0:
                    act.wait_ge(xb_done, 16 * NB * NT)
                A(DT, LEFT[0:DROWS, c % 2, :], ACT.Copy).then_inc(zt_high, 1)

            def mlp(u):
                c, m = u // UNITS, u % UNITS
                act.wait_ge(m_filled, u + 1)
                out = bank[u % 4][:, :]
                if m < 4:
                    at_least(act, m_low, 4 * c + m - 1)
                    A(M1[:, m % 2, :], out, ACT.Relu, bias=B1[:, m:m + 1]).then_inc(m_drained, 1)
                    act.wait_ge(m_drained, u + 1)
                    A(M1H[:, m, :], M1[:, m % 2, :], ACT.Copy).then_inc(m_high, 1)
                elif m < 6:
                    A(M2[:, m - 4, :], out, ACT.Relu, bias=B2[:, m - 4:m - 3]).then_inc(m_drained, 1)
                else:
                    at_least(act, s_y, 16 * c)
                    A(YS, out[0:1, :], ACT.Copy).then_inc(m_drained, 1)
                if m == 4 and c < B // BC - 2:
                    mlp_input(c + 1)

            def tile(t, half, n):
                for k in range(SLOTS):
                    c, j = k // PT, k % PT
                    was = k - ACT_LATE
                    if 1 <= n <= NT:
                        for g in range(NG):
                            if G_AT[g] == was:
                                drain_g(t - 1, g)
                    if n < NT and j == LEFT_AT[c] and (c < CH - 1 or n < NT - 1):
                        drain_left(CH * t + c + 1, c + 1)
                    if 2 <= n and was == L2_OUT:
                        act.wait_ge(l2_filled, t - 1)
                        A(ZT[:, 1, bass.ds((t - 2) * P, P)], gl[:, 0:P], ACT.Copy).then_inc(l2_drained, 1)
                    if 1 <= n <= NT:
                        if k == L1_LAG:
                            drain_h(t - 1, CH - 1)
                        if was in HT_AT:
                            high_ht(t - 1, HT_AT.index(was))
                    if n < NT:
                        for cc in range(CH - 1):
                            if k == PT * (cc + 1) + L1_LAG:
                                drain_h(t, cc)
                        if was in (X1_A, X1_B):
                            high_x1(t, int(was == X1_B))
                    if n < NT - 1:
                        if k == SPLIT:
                            first_part(t + 1, half + n % 2, n + 1)
                        if k == SPLIT + 1:
                            second_part(t + 1, n + 1)
                        if was in (XT_A, XT_B):
                            drain_xt(t + 1, n + 1, int(was == XT_B))
                    if 1 <= n <= NT and k == OUT1_AT:
                        act.wait_ge(g_drained, NG * t)
                        A(ZT[:, 0, bass.ds((t - 1) * P, P)], G[:, F, :], ACT.Copy).then_inc(out1_done, 1)
                    if n < NT:
                        act.wait_ge(z_done, SLOTS * t + k + 1)
                        buffer_free(act, CH * t + c, j)
                        A(ZH[0:rows(j), j, :], Z[0:rows(j), BUFFER[k % len(BUFFER)], :], ACT.Copy).then_inc(zh_done, 1)
                    if n == NT and k == MLP_IN:
                        mlp_input(0)
                    for u, at in enumerate(MLP_AT):
                        if n == NT and at == was:
                            mlp(u)

            act.wait_ge(s_in, 16 * NCONST)
            A(SEL[:, :, :], SELF[:, 0:NPICK + 1, :], ACT.Copy).then_inc(s_cst, 1)
            A(SELX[:, :], SELF[:, NPICK + 1, 0:FX], ACT.Copy).then_inc(s_cst, 1)
            A(IDB[:, :], IDF[:, :], ACT.Copy).then_inc(s_cst, 1)
            act.wait_ge(s_w, 16 * NWEIGHT)
            A(WT2H[:, :, :], WT2S, ACT.Copy).then_inc(s_top, 1)
            A(WTD[:, :], WTDS, ACT.Copy).then_inc(s_top, 1)
            act.wait_ge(s_w0s, 1)
            A(W0H[:, 0:PT, :], W0S[:, 0, :, :], ACT.Copy).then_inc(s_w0h, 1)
            first_part(0, 0, 0)
            second_part(0, 0)
            drain_xt(0, 0, 0)
            drain_xt(0, 0, 1)
            act.wait_ge(s_topl, 2)
            drain_left(0, 0)
            walk(act, tile)
            mlp_input(B // BC - 1)
            for u in range(3 * UNITS, 4 * UNITS):
                mlp(u)

        @block.vector
        def _(dve):
            TT = nc.vector.tensor_tensor

            def first_rest(t, n):
                dve.wait_ge(part_h, t + 1)
                x = X[:, n % 2, :].rearrange("p (f d) -> p d f", d=D)
                TT(x, x, X3[:, :, 0, :], ALU.subtract).then_inc(part_r, 1)

            def last_part(t, n):
                dve.wait_ge(part_m, t + 1)
                TT(X3[:, :, 2, :], X[:, n % 2, :].rearrange("p (f d) -> p d f", d=D), X3[:, :, 1, :],
                   ALU.subtract).then_inc(part_l, 1)

            def low(t, k):
                j = k % PT
                dve.wait_ge(zh_done, SLOTS * t + k + 1)
                buffer_free(dve, CH * t + k // PT, j)
                if j == FULL:
                    r = slice(LH, LH + REST)
                    TT(ZH[r, j, :], Z[r, BUFFER[k % len(BUFFER)], :], ZH[r, j, :].bitcast(F32), ALU.subtract).then_inc(zl_done, 1)
                else:
                    TT(ZL[:, j, :], Z[:, BUFFER[k % len(BUFFER)], :], ZH[:, j, :].bitcast(F32), ALU.subtract).then_inc(zl_done, 1)

            def low_ht(t, q):
                dve.wait_ge(ht_drained, 4 * t + q + 1)
                TT(HTL[:, 4 * q:4 * q + 4, :], two[q % 2][:, :].rearrange("p (g h) -> p g h", h=HID),
                   HTH[:, 4 * q:4 * q + 4, :].bitcast(F32), ALU.subtract).then_inc(ht_low, 1)

            def low_x1(t, part):
                dve.wait_ge(x1_drained, 2 * t + part + 1)
                gs = slice(8 * part, 8 * part + 8)
                TT(X1[:, 1, gs, 0:F], turn[:, 0:8 * FX].rearrange("p (g f) -> p g f", f=FX)[:, :, 0:F],
                   X1[:, 0, gs, 0:F].bitcast(F32), ALU.subtract).then_inc(x1_low, 1)

            def mlp_input(c):
                if c == 0:
                    dve.wait_ge(h_filled, CH * NT)
                    dve.wait_ge(s_top, 3)
                    TT(WT1L, WT1[:, :, :], WT1H.bitcast(F32), ALU.subtract).then_inc(s_topl, 1)
                dve.wait_ge(zt_high, 2 * c + 1)
                TT(ZTL, ZT[:, :, c * BC:(c + 1) * BC], ZTH.bitcast(F32), ALU.subtract).then_inc(zt_low, 1)
                dve.wait_ge(zt_high, 2 * c + 2)
                r = slice(LH, LH + DENSE)
                TT(DT[r, :], LEFT[r, c % 2, :], DT[r, :].bitcast(F32), ALU.subtract).then_inc(zt_low, 1)

            def mlp(u):
                c, m = u // UNITS, u % UNITS
                if m < 4:
                    dve.wait_ge(m_high, 4 * c + m + 1)
                    TT(M1L[:, m, :], M1[:, m % 2, :], M1H[:, m, :].bitcast(F32), ALU.subtract).then_inc(m_low, 1)
                if m == 4 and c < B // BC - 2:
                    mlp_input(c + 1)

            def tile(t, half, n):
                for k in range(SLOTS):
                    c, j = k // PT, k % PT
                    was = k - DVE_LATE
                    if n < NT:
                        if j == 0:
                            dve.wait_ge(left_drained, CH * t + c + 1)
                        if j in SHIFT:
                            dve.wait_ge(moved[j], 32 * (CH * t + c) + 32)
                            other = Z[:, BUFFER[k % len(BUFFER)], :]
                        else:
                            dve.wait_ge(right_filled, NPICK * (CH * t + c) + PICKED.index(j) + 1)
                            other = ring[BANK[j]][0:rows(j), :]
                        at_least(dve, zl_done, SLOTS * t + k + 1 - AGO[k % len(AGO)])
                        TT(Z[0:rows(j), BUFFER[k % len(BUFFER)], :], LEFT[0:rows(j), c % 2, :], other,
                           ALU.mult).then_inc(z_done, 1)
                    if 1 <= n <= NT and was in HT_AT:
                        low_ht(t - 1, HT_AT.index(was))
                    if n < NT and was in (X1_A, X1_B):
                        low_x1(t, int(was == X1_B))
                    if n < NT and k >= ZL_LAG:
                        low(t, k - ZL_LAG)
                    if 1 <= n <= NT and k < ZL_LAG:
                        low(t - 1, k - ZL_LAG + SLOTS)
                    if n < NT - 1:
                        if k == SPLIT:
                            first_rest(t + 1, n + 1)
                        if k == SPLIT + 1:
                            last_part(t + 1, n + 1)
                    if n == NT and k == MLP_IN:
                        mlp_input(0)
                    for u, at in enumerate(MLP_AT):
                        if n == NT and at == was:
                            mlp(u)

            nc.vector.memset(WTDS, 0.0).then_inc(s_zero, 1)
            nc.vector.memset(XB[:, :, :, :, :].bitcast(F32), 0.0).then_inc(s_zero, 1)
            nc.vector.memset(X1[:, 0, :, F:FX].bitcast(F32), 1.0).then_inc(s_zero, 1)
            nc.vector.memset(X1[:, 1, :, F:FX].bitcast(F32), 0.0).then_inc(s_zero, 1)
            dve.wait_ge(s_w, 16 * NWEIGHT)
            TT(W0S[:, 0, :, :], W0S[:, 0, :, :], W0S[:, 1, :, :], ALU.add).then_inc(s_w0s, 1)
            dve.wait_ge(s_top, 2)
            TT(WT2L[:, :, :], WT2S, WT2H[:, :, :].bitcast(F32), ALU.subtract).then_inc(s_topl, 1)
            r = slice(HL, HL + DENSE)
            TT(WTD[r, :], WTDS[r, :], WTD[r, :].bitcast(F32), ALU.subtract).then_inc(s_topl, 1)
            dve.wait_ge(s_w0h, 1)
            TT(W0L[:, 0:PT, :], W0S[:, 0, :, :], W0H[:, 0:PT, :].bitcast(F32), ALU.subtract).then_inc(s_w0l, 1)
            dve.wait_ge(s_w0l, 1)
            r = slice(HL, HL + REST)
            nc.vector.tensor_copy(W0H[r, FULL, :], W0L[r, FULL, :].bitcast(F32)).then_inc(s_w0l, 1)
            first_rest(0, 0)
            last_part(0, 0)
            walk(dve, tile)
            mlp_input(B // BC - 1)
            for u in range(3 * UNITS, 4 * UNITS):
                mlp(u)

        @block.tensor
        def _(pe):
            MM = nc.tensor.matmul

            def turn_x(t, n, part):
                for d in range(8 * part, 8 * part + 8):
                    last = nc.tensor.transpose(turnb[0:NSPLIT, (d % 8) * P:(d % 8 + 1) * P],
                                               X3[:, d, :, :].rearrange("p s f -> p (s f)"), IDB[:, :])
                last.then_inc(xt_filled, 1)

            def select_left(c, cc, n):
                MM(ring[LEFT_BANK][:, :], SEL[:, NPICK, :], XT[:, n % 2, :, DG * cc:DG * cc + DG],
                   start=True, stop=True).then_inc(left_filled, 1)

            def select_right(t, n, k):
                c, j = k // PT, k % PT
                MM(ring[BANK[j]][0:rows(j), :], SEL[:, PICKED.index(j), 0:rows(j)],
                   XT[:, n % 2, :, DG * c:DG * c + DG],
                   start=True, stop=True).then_inc(right_filled, 1)

            def layer1(t, k):
                c, j = k // PT, k % PT
                s = k % PT
                pe.wait_ge(zl_done, SLOTS * t + k + 1)
                if j == 0:
                    at_least(pe, h_drained, CH * t + c - 1)
                out = acc[c % 2][:, :]
                if j == FULL:
                    MM(out, W0H[0:RROWS, j, :], ZH[0:RROWS, s, :], start=False, stop=True).then_inc(h_filled, 1)
                else:
                    MM(out, W0H[:, j, :], ZH[:, s, :], start=(j == 0), stop=False)
                    MM(out, W0H[:, j, :], ZL[:, s, :], start=False, stop=False)
                    MM(out, W0L[:, j, :], ZH[:, s, :], start=False, stop=False).then_inc(z_used, 1)

            pe.wait_ge(part_l, 1)
            pe.wait_ge(s_cst, 3)
            turn_x(0, 0, 0)
            pe.wait_ge(xt_drained, 1)
            turn_x(0, 0, 1)
            pe.wait_ge(xt_drained, 1)
            select_left(0, 0, 0)
            pe.wait_ge(s_w0l, 2)
            pe.wait_ge(s_w, 16 * NWEIGHT)

            def mlp(u):
                c, m = u // UNITS, u % UNITS
                cols = slice(c * BC, (c + 1) * BC)
                at_least(pe, m_drained, u - 3)
                out = bank[u % 4][:, :]
                if m < 4:
                    ms = slice(m * P, (m + 1) * P)
                    if m == 0:
                        pe.wait_ge(s_topl, 3)
                        pe.wait_ge(zt_low, 2 * c + 2)
                    for q in range(2):
                        MM(out, WT1H[:, q, ms], ZTH[:, q, :], start=(q == 0), stop=False)
                        MM(out, WT1H[:, q, ms], ZTL[:, q, :], start=False, stop=False)
                        MM(out, WT1L[:, q, ms], ZTH[:, q, :], start=False, stop=False)
                    MM(out, WTD[:, ms], DT, start=False, stop=True).then_inc(m_filled, 1)
                elif m < 6:
                    ms = slice((m - 4) * P, (m - 3) * P)
                    for q in range(TOP1 // P):
                        if m == 4:
                            pe.wait_ge(m_low, 4 * c + q + 1)
                        MM(out, WT2H[:, q, ms], M1H[:, q, :], start=(q == 0), stop=False)
                        MM(out, WT2H[:, q, ms], M1L[:, q, :], start=False, stop=False)
                        last = MM(out, WT2L[:, q, ms], M1H[:, q, :], start=False, stop=(q == TOP1 // P - 1))
                    last.then_inc(m_filled, 1)
                else:
                    pe.wait_ge(m_drained, UNITS * c + 6)
                    for q in range(TOP2 // P):
                        last = MM(out[0:1, :], WT3[:, q:q + 1], M2[:, q, :], start=(q == 0), stop=(q == 1))
                    last.then_inc(m_filled, 1)

            def tile(t, half, n):
                for k in range(SLOTS):
                    c, j = k // PT, k % PT
                    C = CH * t + c
                    if n < NT:
                        if j == LEFT_AT[c] and (c < CH - 1 or n < NT - 1):
                            pe.wait_ge(left_drained, C + 1)
                            if c == 1:
                                pe.wait_ge(xt_drained, 2 * t + 2)
                            if c == CH - 1:
                                pe.wait_ge(xt_drained, 2 * t + 3)
                                select_left(C + 1, 0, n + 1)
                            else:
                                select_left(C + 1, c + 1, n)
                        if j in PICKED:
                            at_least(pe, z_done, PT * C + FREE[j])
                        if j in PICKED:
                            select_right(t, n, k)
                    if n < NT and k >= L1_LAG:
                        layer1(t, k - L1_LAG)
                    if 1 <= n <= NT and k < L1_LAG:
                        layer1(t - 1, k - L1_LAG + SLOTS)
                    for m, at in enumerate(L2_AT):
                        if (1 <= n <= NT and at == k) or (2 <= n and at == k + SLOTS):
                            if m == 0:
                                pe.wait_ge(g_drained, NG * t)
                            n0, n1 = F * m // len(L2_AT), F * (m + 1) // len(L2_AT)
                            for f in range(n0, n1):
                                last = MM(gl[:, 0:P], W1[:, f, :], G[:, f, :], start=(f == 0), stop=(f == F - 1))
                            if n1 == F:
                                last.then_inc(l2_filled, 1)
                    if 1 <= n <= NT and k in HT_AT:
                        q = HT_AT.index(k)
                        if q == 0:
                            pe.wait_ge(h_drained, CH * t)
                            pe.wait_ge(x1_low, 2 * t)
                        elif q == 1:
                            at_least(pe, l2_drained, t - 1)
                        else:
                            pe.wait_ge(ht_low, 4 * (t - 1) + q - 1)
                        for g in range(4 * q, 4 * q + 4):
                            last = nc.tensor.transpose(two[q % 2][:, (g % 4) * HID:(g % 4 + 1) * HID],
                                                       H[:, NB * g:NB * g + NB, :].rearrange("p b d -> p (b d)"), IDF[:, :])
                        last.then_inc(ht_filled, 1)
                    for g in range(NG):
                        if not (1 <= n <= NT and G_AT[g] == k):
                            continue
                        if g % 4 == 0:
                            pe.wait_ge(ht_low, 4 * (t - 1) + g // 4 + 1)
                        if g == 0:
                            pe.wait_ge(xb_done, 16 * NB * t)
                            pe.wait_ge(ht_low, 4 * t - 1)
                        elif g == 1:
                            pe.wait_ge(ht_low, 4 * t)
                        else:
                            pe.wait_ge(g_drained, NG * (t - 1) + g - 1)
                        out = two[g % 2][:, 0:FX * NB]
                        MM(out, HTH[:, g, :], XB[:, 0, :, g, :], start=True, stop=False)
                        MM(out, HTH[:, g, :], XB[:, 1, :, g, :], start=False, stop=False)
                        MM(out, HTL[:, g, :], XB[:, 0, :, g, :], start=False, stop=True).then_inc(g_filled, 1)
                    if n < NT - 1 and k in (XT_A, XT_B):
                        if k == XT_A:
                            pe.wait_ge(part_l, t + 2)
                            if n > 0:
                                pe.wait_ge(g_drained, NG * t - 1)
                            else:
                                pe.wait_ge(xt_drained, 2)
                        else:
                            pe.wait_ge(x1_low, 2 * t + 1)
                        turn_x(t + 1, n + 1, int(k == XT_B))
                    if n < NT and k in (X1_A, X1_B):
                        part = int(k == X1_B)
                        if n < NT - 1:
                            pe.wait_ge(xt_drained, 2 * t + 3 + part)
                        elif part:
                            pe.wait_ge(x1_low, 2 * t + 1)
                        else:
                            pe.wait_ge(g_drained, NG * t - 1)
                        for g in range(8 * part, 8 * part + 8):
                            last = MM(turn[:, (g % 8) * FX:(g % 8 + 1) * FX], XT[:, n % 2, NB * g:NB * g + NB, :].rearrange("p b d -> p (b d)"),
                                      SELX[:, :], start=True, stop=True)
                        last.then_inc(x1_filled, 1)
                    for u, at in enumerate(MLP_AT):
                        if n == NT and at == k:
                            if u == 0:
                                pe.wait_ge(z_done, SLOTS * NT)
                            mlp(u)

            walk(pe, tile)
            for u in range(3 * UNITS, 4 * UNITS):
                mlp(u)


def kernel(**inputs):
    import concourse.bacc as bacc
    from concourse.bass_utils import run_bass_kernel_spmd

    left, right = pair_tables()
    arrays = {}

    def lay(name, a):
        arrays[name] = np.ascontiguousarray(a)

    lay("ids", inputs["ids"])
    for f in range(F):
        lay(f"tbl_{f}", inputs[f"tbl_{f}"])
    wanted = np.full((NPICK + 2, P), -1)
    wanted[:NPICK] = [right[t] for t in PICKED]
    wanted[NPICK] = left
    wanted[NPICK + 1, :F] = np.arange(F)
    sel = (np.arange(NSPLIT)[:, None, None] % F == wanted[None]).astype(np.float32)
    lay("sel", sel.reshape(NSPLIT, -1))
    lay("ident", np.eye(P, dtype=np.float32))
    w0 = np.asarray(inputs["L0_rec_W0"]).reshape(HID, F, F)
    pad = np.zeros((HID, F + 1, F + 1), w0.dtype)
    pad[:, :F, :F] = w0
    ll = np.broadcast_to(np.array(left), (PT, P))
    rr = np.array(right)
    li = np.where(rr < 0, F, ll)
    ri = np.where(rr < 0, F, rr)
    lay("w0a", pad[:, li, ri].transpose(2, 1, 0).reshape(P, -1))
    same = li == ri
    lay("w0b", pad[:, np.where(same, F, ri), np.where(same, F, li)].transpose(2, 1, 0).reshape(P, -1))
    lay("w1t", np.asarray(inputs["L0_rec_W1"]).reshape(HID, F, HID).transpose(2, 1, 0).reshape(HID, F * HID))
    lay("wt1", inputs["W_top1"])
    lay("wt2", inputs["W_top2"])
    lay("wt3", np.asarray(inputs["W_top3"]).reshape(TOP2 // P, P).T)
    lay("b1", np.asarray(inputs["b_top1"]).reshape(TOP1 // P, P).T)
    lay("b2", np.asarray(inputs["b_top2"]).reshape(TOP2 // P, P).T)
    lay("denset", np.asarray(inputs["dense_ctx"]).T)

    nc = bacc.Bacc("TRN2", target_bir_lowering=False, num_devices=1)
    ap = {k: nc.dram_tensor(k, a.shape, mybir.dt.from_np(a.dtype), kind="ExternalInput").ap()
          for k, a in arrays.items()}
    y = nc.dram_tensor("y", (1, B), F32, kind="ExternalOutput").ap()
    dlrm(nc, ap["ids"], [ap[f"tbl_{f}"] for f in range(F)], ap["sel"], ap["ident"],
         ap["w0a"], ap["w0b"], ap["w1t"], ap["wt1"], ap["b1"], ap["wt2"], ap["b2"], ap["wt3"], ap["denset"], y)
    out = run_bass_kernel_spmd(nc, [arrays], core_ids=[0]).results[0]["y"]
    return out.reshape(B, 1)
```
